# Optimizing a Trainium2 kernel written in Bass

```python
import numpy as np
import jax
import jax.numpy as jnp

def _softmax(x, axis=-1):
    return jax.nn.softmax(x, axis=axis)

def _gelu(x):
    return jax.nn.gelu(x, approximate=True)

def _silu(x):
    return jax.nn.silu(x)

def _sigmoid(x):
    return jax.nn.sigmoid(x)

def _layernorm(x, axis=-1, eps=1e-05):
    m = jnp.mean(x, axis=axis, keepdims=True)
    v = jnp.var(x, axis=axis, keepdims=True)
    return (x - m) / jnp.sqrt(v + eps)

def _scatter_add(tgt, idx, src, axis=0):
    return tgt.at[idx].add(src)

def _segment_sum(src, seg, n):
    return jax.ops.segment_sum(src, seg, n)
kernel_name = 'mk_prb_d1_jaxref_r8_f4b245'

def setup_inputs(seed: int=0):
    np.random.seed(seed)
    _w = jnp.asarray

    def _L0_attn_setup():
        import jax, jax.numpy as jnp
        import numpy as np
        from jax import lax
        B, N, DIM = (2, 256, 128)
        HEADS, DHEAD = (16, 64)
        NUM_MEM_KV = 16
        SPARSE_TOPK = 64
        INNER = HEADS * DHEAD
        key = jax.random.key(seed)
        ks = jax.random.split(key, 10)
        s = 0.02
        return {'x': jax.random.normal(ks[0], (B, N, DIM), dtype=jnp.float32), 'Wq': jax.random.normal(ks[1], (DIM, INNER), dtype=jnp.float32) * s, 'Wk': jax.random.normal(ks[2], (DIM, INNER), dtype=jnp.float32) * s, 'Wv': jax.random.normal(ks[3], (DIM, INNER), dtype=jnp.float32) * s, 'pre_proj': jax.random.normal(ks[4], (HEADS, HEADS), dtype=jnp.float32), 'post_proj': jax.random.normal(ks[5], (HEADS, HEADS), dtype=jnp.float32), 'mem_k': jax.random.normal(ks[6], (HEADS, NUM_MEM_KV, DHEAD), dtype=jnp.float32), 'mem_v': jax.random.normal(ks[7], (HEADS, NUM_MEM_KV, DHEAD), dtype=jnp.float32), 'Wo': jax.random.normal(ks[8], (INNER, DIM), dtype=jnp.float32) * s, 'bo': jnp.zeros((DIM,), dtype=jnp.float32)}
    _L0_attn_in = _L0_attn_setup()

    def _L0_ffn_setup():
        import jax, jax.numpy as jnp
        import numpy as np
        HIDDEN = 128
        MOE_FF = 64
        SHARED_FF = 352
        NUM_EXPERTS = 16
        TOP_K = 2
        NORM_TOPK = True
        key = jax.random.key(seed)
        ks = jax.random.split(key, 8)
        s = 0.02
        return {'layer_input': jax.random.normal(ks[0], (1, 256, HIDDEN), dtype=jnp.float32), 'gate_w': jax.random.normal(ks[1], (NUM_EXPERTS, HIDDEN), dtype=jnp.float32) * s, 'w_gate_up': jax.random.normal(ks[2], (NUM_EXPERTS, HIDDEN, 2 * MOE_FF), dtype=jnp.float32) * s, 'w_down': jax.random.normal(ks[3], (NUM_EXPERTS, MOE_FF, HIDDEN), dtype=jnp.float32) * s, 'shared_w_gate': jax.random.normal(ks[4], (SHARED_FF, HIDDEN), dtype=jnp.float32) * s, 'shared_w_up': jax.random.normal(ks[5], (SHARED_FF, HIDDEN), dtype=jnp.float32) * s, 'shared_w_down': jax.random.normal(ks[6], (HIDDEN, SHARED_FF), dtype=jnp.float32) * s, 'shared_gate_w': jax.random.normal(ks[7], (1, HIDDEN), dtype=jnp.float32) * s}
    _L0_ffn_in = _L0_ffn_setup()
    _d = {'L0_attn_x': _L0_attn_in['x'], 'L0_attn_Wq': _L0_attn_in['Wq'], 'L0_attn_Wk': _L0_attn_in['Wk'], 'L0_attn_Wv': _L0_attn_in['Wv'], 'L0_attn_pre_proj': _L0_attn_in['pre_proj'], 'L0_attn_post_proj': _L0_attn_in['post_proj'], 'L0_attn_mem_k': _L0_attn_in['mem_k'], 'L0_attn_mem_v': _L0_attn_in['mem_v'], 'L0_attn_Wo': _L0_attn_in['Wo'], 'L0_attn_bo': _L0_attn_in['bo'], 'L0_ffn_gate_w': _L0_ffn_in['gate_w'], 'L0_ffn_w_gate_up': _L0_ffn_in['w_gate_up'], 'L0_ffn_w_down': _L0_ffn_in['w_down'], 'L0_ffn_shared_w_gate': _L0_ffn_in['shared_w_gate'], 'L0_ffn_shared_w_up': _L0_ffn_in['shared_w_up'], 'L0_ffn_shared_w_down': _L0_ffn_in['shared_w_down'], 'L0_ffn_shared_gate_w': _L0_ffn_in['shared_gate_w']}
    _x0 = _d['L0_attn_x']
    _d['L0_attn_x'] = jax.random.normal(jax.random.fold_in(jax.random.key(seed), 1), (1, 2048, 128), dtype=_x0.dtype)
    del _x0
    return _d

def reference(L0_attn_x, L0_attn_Wq, L0_attn_Wk, L0_attn_Wv, L0_attn_pre_proj, L0_attn_post_proj, L0_attn_mem_k, L0_attn_mem_v, L0_attn_Wo, L0_attn_bo, L0_ffn_gate_w, L0_ffn_w_gate_up, L0_ffn_w_down, L0_ffn_shared_w_gate, L0_ffn_shared_w_up, L0_ffn_shared_w_down, L0_ffn_shared_gate_w):

    def _L0_attn_ref(x, Wq, Wk, Wv, pre_proj, post_proj, mem_k, mem_v, Wo, bo):
        import jax, jax.numpy as jnp
        import numpy as np
        from jax import lax
        B, N, DIM = (2, 256, 128)
        HEADS, DHEAD = (16, 64)
        NUM_MEM_KV = 16
        SPARSE_TOPK = 64
        INNER = HEADS * DHEAD
        b, n, _ = x.shape
        h, m, d = mem_k.shape
        scale = d ** (-0.5)

        def split_heads(t):
            return t.reshape(b, n, h, d).transpose(0, 2, 1, 3)
        q = split_heads(x @ Wq)
        k = split_heads(x @ Wk)
        v = split_heads(x @ Wv)
        k = jnp.concatenate([jnp.broadcast_to(mem_k[None], (b, h, m, d)), k], axis=2)
        v = jnp.concatenate([jnp.broadcast_to(mem_v[None], (b, h, m, d)), v], axis=2)
        dots = jnp.einsum('bhid,bhjd->bhij', q, k) * scale
        neg = -jnp.finfo(dots.dtype).max
        dots = jnp.einsum('bhij,hk->bkij', dots, pre_proj)
        j = m + n
        ii = jnp.arange(n)[:, None]
        jj = jnp.arange(j)[None, :]
        causal = jj - m > ii
        dots = jnp.where(causal[None, None], neg, dots)
        top = lax.top_k(dots, SPARSE_TOPK)[0]
        vk = top[..., -1:]
        dots = jnp.where(dots < vk, neg, dots)
        attn = jax.nn.softmax(dots, axis=-1)
        attn = jnp.einsum('bhij,hk->bkij', attn, post_proj)
        out = jnp.einsum('bhij,bhjd->bhid', attn, v)
        out = out.transpose(0, 2, 1, 3).reshape(b, n, h * d)
        return out @ Wo + bo

    def _L0_ffn_ref(layer_input, gate_w, w_gate_up, w_down, shared_w_gate, shared_w_up, shared_w_down, shared_gate_w):
        import jax, jax.numpy as jnp
        import numpy as np
        HIDDEN = 128
        MOE_FF = 64
        SHARED_FF = 352
        NUM_EXPERTS = 16
        TOP_K = 2
        NORM_TOPK = True
        B, S, D = layer_input.shape
        x = layer_input.reshape(-1, D)
        N = x.shape[0]
        shared = jax.nn.silu(x @ shared_w_gate.T) * (x @ shared_w_up.T) @ shared_w_down.T
        shared = shared * jax.nn.sigmoid(x @ shared_gate_w.T)
        logits = x @ gate_w.T
        probs = jax.nn.softmax(logits.astype(jnp.float32), axis=-1)
        rw, sel = jax.lax.top_k(probs, TOP_K)
        if NORM_TOPK:
            rw = rw / rw.sum(axis=-1, keepdims=True)
        rw = rw.astype(x.dtype)
        combine = jnp.zeros((N, NUM_EXPERTS), x.dtype).at[jnp.arange(N)[:, None], sel].set(rw)
        gu = jnp.einsum('nd,edf->nef', x, w_gate_up)
        g, h = jnp.split(gu, 2, axis=-1)
        h = jax.nn.silu(g) * h
        expert_out = jnp.einsum('nef,efd,ne->nd', h, w_down, combine)
        out = expert_out + shared
        return out.reshape(B, S, D)
    x = L0_attn_x
    xn = _layernorm(x, axis=-1)
    x = x + _L0_attn_ref(xn, L0_attn_Wq, L0_attn_Wk, L0_attn_Wv, L0_attn_pre_proj, L0_attn_post_proj, L0_attn_mem_k, L0_attn_mem_v, L0_attn_Wo, L0_attn_bo) + _L0_ffn_ref(xn, L0_ffn_gate_w, L0_ffn_w_gate_up, L0_ffn_w_down, L0_ffn_shared_w_gate, L0_ffn_shared_w_up, L0_ffn_shared_w_down, L0_ffn_shared_gate_w)
    return x

_drawn_inputs = setup_inputs


def setup_inputs(seed=0):
    import zlib

    import numpy as np

    out = dict(_drawn_inputs(seed))
    spreads = {'L0_attn_bo': (0.0, 0.362)}
    factors = {'L0_ffn_gate_w': 8.0,
     'L0_ffn_w_gate_up': 8.0,
     'L0_ffn_w_down': 8.0,
     'L0_ffn_shared_w_gate': 8.0,
     'L0_ffn_shared_w_up': 8.0,
     'L0_ffn_shared_w_down': 8.0,
     'L0_ffn_shared_gate_w': 8.0}
    for name, (base, spread) in spreads.items():
        noise = np.random.default_rng([zlib.crc32(name.encode()), seed]).standard_normal(out[name].shape)
        drawn = base * np.exp(spread * noise) if base else spread * noise
        out[name] = jnp.asarray(drawn.astype(out[name].dtype))
    for name, factor in factors.items():
        out[name] = (out[name] * factor).astype(out[name].dtype)
    return out
```

```python
import math
from contextlib import ExitStack

import concourse.bass as bass
from concourse import mybir

F32 = mybir.dt.float32
BF16 = mybir.dt.bfloat16
I32 = mybir.dt.int32
ALU = mybir.AluOpType
ACT = mybir.ActivationFunctionType
AXX = mybir.AxisListType.X

N = 2048
D = 128
P = 128
NB = N // P
HEADS = 16
DH = 64
MEM = 16
TOPK = 64
NCH = HEADS * DH // P
INNER = HEADS * DH
EXPERTS = 16
FF = 64
SHARED = 352
NPAIR = EXPERTS // 2
SBLK = [(0, 128), (128, 128), (256, 96)]
NJ = NPAIR + len(SBLK)
EPS = 1e-5
SCALE_BITS = 40
DOWN = 2.0 ** -SCALE_BITS
UP = 2.0 ** SCALE_BITS
MASKED = -(2.0 ** 40)
LOWEST = -3.0e38
QUADS = NB * 4
WMAX = N + MEM
PIECE = 1024
NBLK = NB + 1
FIRST = 4
AIM = 60.3
LOW_C, HIGH_C = 56, 64


def width(q):
    return P * (q // 4 + 1) + MEM


def pieces(q):
    w = width(q)
    return [(a, min(a + PIECE, w)) for a in range(0, w, PIECE)]


def tpieces(q):
    nb = q // 4 + 2
    return [(a, min(a + 4, nb)) for a in range(0, nb, 4)]


def ring_items():
    items = []
    for p in range(-1, QUADS + 3):
        if p == -1:
            items.append(("query", 0))
            continue
        if needs_search(p) or needs_search(p - 2):
            items.append(("small", p))
        for h in range(4):
            if h == 2 and 0 <= p - 3 < QUADS:
                items.append(("out", p - 3))
            if p < QUADS:
                items += [("score", 4 * p + h, i) for i in range(len(pieces(p)))]
            if h == 1 and p + 1 < QUADS:
                items.append(("query", p + 1))
    return items


def needs_search(q):
    return FIRST <= q < QUADS


RING = {item: i for i, item in enumerate(ring_items())}


def tcount(n):
    return sum(4 * len(tpieces(q)) for q in range(n // 4)) + (n % 4 + 1) * len(tpieces(n // 4))


def build(nc, x, wq, wk, wv, pre, post, mem_k, mem_v, wo, bo, gate_w, w_gu, w_down, s_gate, s_up, s_down,
          s_gw, ident_d, sel_d, cmask_d, nz_d, kap_d, iota_d, out):
    ctx = ExitStack()
    with ctx:
        def sb(name, shape, dt=F32):
            return ctx.enter_context(nc.sbuf_tensor(name, shape, dt))

        def sem(name):
            return ctx.enter_context(nc.semaphore(name))

        S = sb("S", [P, 8, WMAX])
        E = sb("E", [P, 3, WMAX])
        Y = sb("Y", [P, WMAX])
        junk = sb("junk", [P, 2, WMAX], BF16)
        PT = sb("PT", [P, 2, NBLK * P])
        xnT = sb("xnT", [P, N])
        XN = sb("XN", [P, NB, D])
        M = sb("M", [P, HEADS * D])
        PV = sb("PV", [P, HEADS * D])
        MV = sb("MV", [MEM, HEADS * D])
        Kmem = sb("Kmem", [P, HEADS * MEM])
        acc = sb("acc", [P, NB, D])
        QT = sb("QT", [P, 2, 4 * P])
        sq = sb("sq", [P, 4 * P])
        zst = sb("zst", [P, 4 * P])
        ident = sb("ident", [P, P])
        identb = sb("identb", [P, P], BF16)
        cmask = sb("cmask", [P, P])
        cmaskb = sb("cmaskb", [P, P], BF16)
        ones = sb("ones", [P, 1])
        half = sb("half", [P, 4])
        minus1 = sb("minus1", [P, 4])
        iota = sb("iota", [P, 4, 9])
        nz = sb("nz", [P, NB])
        kap = sb("kap", [P, NB])
        mxp = sb("mxp", [P, 8, 3])
        mxq = sb("mxq", [P, 2, 4])
        mbias = sb("mbias", [P, 2, 4])
        sg2 = sb("sg2", [P, 2, 4])
        nt = sb("nt", [P, 2, 4, 4])
        g = sb("g", [P, 2, 3, 4])
        w8 = sb("w8", [P, 16, 4])
        cnt = sb("cnt", [P, 2, 4])
        rank = sb("rank", [P, 4])
        hot = sb("hot", [P, 2, 4, 9])
        off = sb("off", [P, 4])
        fail = sb("fail", [P, 4])
        failed = sb("failed", [1, 5], I32)
        y9 = sb("y9", [P, 2, 4, 9])
        t8 = sb("t8", [P, 8])
        pick = sb("pick", [P, 9])
        thr = sb("thr", [P, 8])
        rsum = sb("rsum", [P, 8])
        rinv = sb("rinv", [P, 2, 4])
        memPT = sb("memPT", [MEM, 2, 4, P])
        st = sb("st", [P, 8, NB])

        Sf = S[:, :, :].rearrange("p a b -> p (a b)")
        Ef = E[:, :, :].rearrange("p a b -> p (a b)")
        PTf = PT[:, :, :].rearrange("p a b -> p (a b)")
        wqkv = Sf[:, 0:3 * INNER].rearrange("p (t n) -> p t n", t=3)
        wT = Sf[:, 3072:3072 + 3 * INNER].rearrange("p (t c n) -> p t c n", t=3, c=NCH)
        woS = Sf[:, 6144:7168].rearrange("p (c n) -> p c n", c=NCH)
        memS = Sf[:, 7168:7424].rearrange("p (t n) -> p t n", t=2)
        memT = Sf[:, 7424:7680].rearrange("p (t c m) -> p t c m", t=2, c=NCH)
        preB = Sf[:, 7680:7808].rearrange("p (c k) -> p c k", c=NCH)
        postB = Sf[:, 7808:7936].rearrange("p (c k) -> p c k", c=NCH)
        preS = Sf[0:HEADS, 7936:7952]
        postS = Sf[0:HEADS, 7952:7968]
        postT = Sf[0:HEADS, 7968:7984]
        gateS = Sf[0:EXPERTS + 1, 7984:8112]
        gateT = Sf[:, 8112:8129]
        sel = Sf[0:EXPERTS + 1, 8192:8192 + 9 * P].rearrange("p (c n) -> p c n", c=9)
        wg = Sf[:, 9344:10368].rearrange("p (e f) -> p e f", e=EXPERTS)
        wu = Sf[:, 10368:11392].rearrange("p (e f) -> p e f", e=EXPERTS)
        wd = Sf[:, 11392:12416].rearrange("p (c n) -> p c n", c=NPAIR)
        shS = Sf[:, 12416:12416 + 6 * P].rearrange("p (t b n) -> p t b n", t=2, b=3)
        shT = Sf[:, 13184:13184 + 6 * P].rearrange("p (t b n) -> p t b n", t=2, b=3)
        sdS = Sf[:, 13952:13952 + SHARED]
        sdT = Sf[:, 14304:14304 + 3 * P].rearrange("p (b n) -> p b n", b=3)
        lg = Sf[:, 14688:14688 + NB * 17].rearrange("p (b e) -> p b e", b=NB)
        comb = Sf[:, 14960:14960 + NB * 17].rearrange("p (b e) -> p b e", b=NB)
        rt = Sf[:, 15232:15232 + 4 * NB * EXPERTS].rearrange("p (t b e) -> p t b e", t=4, b=NB)
        scaled = Ef[:, 0:4096].rearrange("p (t k n) -> p t k n", t=2, k=HEADS)
        scaledm = Ef[:, 4096:4608].rearrange("p (t k m) -> p t k m", t=2, k=HEADS)
        bob = Ef[:, 4608:4736]
        H = Ef[:, 0:5632].rearrange("p (j n) -> p j n", j=NJ)
        sg = PTf[:, 0:1024].rearrange("p (t n) -> p t n", t=2)
        su = PTf[:, 1024:2048].rearrange("p (t n) -> p t n", t=2)
        combT = Y[0:EXPERTS + 1, 0:N]
        xsq = PTf[:, 2048:4096].rearrange("p (b d) -> p b d", b=NB)

        R = [ctx.enter_context(nc.psum_tensor(f"R{i}", [P, PIECE], F32)) for i in range(2)]
        T = [ctx.enter_context(nc.psum_tensor(f"T{i}", [P, 512], F32)) for i in range(3)]
        Z = ctx.enter_context(nc.psum_tensor("Z", [P, 512], F32))

        x_loaded, consts_loaded, att_loaded, ffn_loaded = (sem(s) for s in (
            "x_loaded", "consts_loaded", "att_loaded", "ffn_loaded"))
        ones_set = sem("ones_set")
        casts_done = sem("casts_done")
        var_ready = sem("var_ready")
        std_ready = sem("std_ready")
        xn_ready = sem("xn_ready")
        tr_full, tr_taken = sem("tr_full"), sem("tr_taken")
        mixB_full, mixB_taken = sem("mixB_full"), sem("mixB_taken")
        scaled_ready, scaled_used = sem("scaled_ready"), sem("scaled_used")
        prod_taken = sem("prod_taken")
        gates_full, comb_ready = sem("gates_full"), sem("comb_ready")
        gates_taken = sem("gates_taken")
        gexp_ready, gexp_done = sem("gexp_ready"), sem("gexp_done")
        ct_full, ct_taken = sem("ct_full"), sem("ct_taken")
        gu_full, gate_read, h_ready = sem("gu_full"), sem("gate_read"), sem("h_ready")
        down_full, down_taken = sem("down_full"), sem("down_taken")
        dve_chain, pool_chain = sem("dve_chain"), sem("pool_chain")
        t_banks_zeroed = sem("t_banks_zeroed")

        ring_full, ring_taken = sem("ring_full"), sem("ring_taken")
        tp_full, tp_taken = sem("tp_full"), sem("tp_taken")
        z_done, z_taken = sem("z_done"), sem("z_taken")
        exp_done = sem("exp_done")
        signs_summed = sem("signs_summed")
        squares_ready = sem("squares_ready")
        step_ready = sem("step_ready")
        counted = sem("counted")
        ranks_ready = sem("ranks_ready")
        max_ready = sem("max_ready")
        probs_ready = sem("probs_ready")
        rows_ready = sem("rows_ready")
        general_chain = sem("general_chain")
        stored = sem("stored")
        mem_kept = sem("mem_kept")

        blocks = []
        for t in range(3):
            for c0 in range(0, NCH, 4):
                blocks.append(([(wqkv[:, t, (c0 + i) * P:(c0 + i + 1) * P], P, P) for i in range(4)],
                               wT[:, t, c0:c0 + 4, :].rearrange("p c n -> p (c n)"), P, 512))
        blocks.append(([(memS[:, t, :], P, P) for t in range(2)],
                       memT[:, :, :, :].rearrange("p t c m -> p (t c m)"), P, 256))
        blocks.append(([(postS, HEADS, HEADS)], postT, HEADS, HEADS))
        n_att_tr = len(blocks)
        blocks.append(([(gateS, EXPERTS + 1, P)], gateT, P, EXPERTS + 1))
        for t in range(2):
            blocks.append(([(shS[0:n, t, b, :], n, P) for b, (_, n) in enumerate(SBLK)],
                           shT[:, t, :, :].rearrange("p b n -> p (b n)")[:, 0:SHARED], P, SHARED))
        for b, (a, n) in enumerate(SBLK):
            blocks.append(([(sdS[:, a:a + n], P, n)], sdT[0:n, b, :], n, P))
        n_w_tr = len(blocks)
        for b in range(0, NB, 4):
            blocks.append(([(XN[:, b + i, :], P, P) for i in range(4)], xnT[:, b * P:(b + 4) * P], P, 512))
        n_tr = len(blocks)

        block = ctx.enter_context(nc.Block())

        @block.sync
        def _(sp):
            sp.dma_start(acc[:, :, :], x.rearrange("(b p) d -> p b d", p=P)).then_inc(x_loaded, 16)
            for t, w in enumerate((wq, wk, wv)):
                sp.dma_start(wqkv[:, t, :], w).then_inc(att_loaded, 16)
            sp.dma_start(woS, wo.rearrange("(c p) n -> p c n", p=P)).then_inc(att_loaded, 16)
            sp.dma_start(preS, pre).then_inc(att_loaded, 16)
            sp.dma_start(postS, post).then_inc(att_loaded, 16)
            for t, m in enumerate((mem_k, mem_v)):
                for c in range(NCH):
                    sp.dma_start(memS[c * MEM:(c + 1) * MEM, t, :].rearrange("m (t e) -> m t e", t=2),
                                 m[2 * c:2 * c + 2].rearrange("t m e -> m t e")).then_inc(att_loaded, 16)
            for b in range(NB):
                sp.wait_ge(rows_ready, b + 1)
                sp.dma_start(out[b * P:(b + 1) * P, :], acc[:, b, :]).then_inc(stored, 16)
            sp.wait_ge(stored, 16 * NB)

        @block.gpsimd
        def _(pool):
            chain = [0]

            def link(ins):
                chain[0] += 1
                ins.then_inc(pool_chain, 1)
                pool.wait_ge(pool_chain, chain[0])

            nc.gpsimd.memset(ones[:], 1.0).then_inc(ones_set, 1)
            nc.gpsimd.memset(half[:], 0.5).then_inc(ones_set, 1)
            nc.gpsimd.memset(minus1[:], -1.0).then_inc(ones_set, 1)
            pool.wait_ge(ones_set, 3)

            def w(i):
                return w8[:, i, :]

            def start(q):
                pool.wait_ge(ring_taken, RING["query", q] + 1)
                if q > FIRST:
                    pool.wait_ge(ring_full, RING["small", q - 1] + 1)
                nc.gpsimd.tensor_tensor(sq[:], QT[:, q % 2, :], QT[:, q % 2, :], ALU.mult).then_inc(squares_ready, 1)

            def first_threshold(q):
                b, r = q % 2, q // 4
                pool.wait_ge(ring_taken, RING["small", q] + 1)
                link(nc.gpsimd.tensor_tensor(w(0), sg2[:, b, :], half[:], ALU.pow))
                link(nc.gpsimd.tensor_scalar(w(1), w(0), kap[:, r:r + 1], None, ALU.mult))
                nc.gpsimd.tensor_scalar(nt[:, b, 0, :], w(0), nz[:, r:r + 1], None, ALU.mult).then_inc(step_ready, 1)
                pool.wait_ge(step_ready, 4 * (q - FIRST) + 1)

            def miss(q, s, to):
                wd_ = width(q)
                link(nc.gpsimd.tensor_scalar(w(2), g[:, q % 2, s, :], float(LOW_C + HIGH_C - wd_), None, ALU.subtract))
                link(nc.gpsimd.tensor_tensor(w(2), w(2), w(2), ALU.mult))
                link(nc.gpsimd.tensor_scalar(w(2), w(2), (HIGH_C - LOW_C + 0.5) ** 2, None, ALU.is_gt))
                link(nc.gpsimd.tensor_scalar(w(to), g[:, q % 2, s, :], float(2 * AIM - wd_), None, ALU.subtract))
                link(nc.gpsimd.tensor_tensor(w(3), w(to), w(2), ALU.mult))

            def move(q, s):
                b = q % 2
                link(nc.gpsimd.tensor_tensor(w(3), w(3), w(5), ALU.mult))
                nc.gpsimd.tensor_tensor(nt[:, b, s + 1, :], nt[:, b, s, :], w(3), ALU.subtract).then_inc(step_ready, 1)
                pool.wait_ge(step_ready, 4 * (q - FIRST) + s + 2)

            def slope(dt, dg):
                link(nc.gpsimd.tensor_tensor(w(5), dt, dg, ALU.mult))
                link(nc.gpsimd.tensor_tensor(w(4), dg, dg, ALU.mult))
                link(nc.gpsimd.tensor_scalar(w(4), w(4), 1.0, None, ALU.max))
                link(nc.gpsimd.tensor_tensor(w(4), w(4), minus1[:], ALU.pow))
                link(nc.gpsimd.tensor_tensor(w(5), w(5), w(4), ALU.mult))

            def step(q, s):
                b = q % 2
                pool.wait_ge(signs_summed, 4 * (3 * (q - FIRST) + s + 1))
                if s == 0:
                    miss(q, 0, 6)
                    link(nc.gpsimd.tensor_copy(w(5), w(1)))
                    move(q, 0)
                elif s == 1:
                    miss(q, 1, 7)
                    link(nc.gpsimd.tensor_tensor(w(8), nt[:, b, 1, :], nt[:, b, 0, :], ALU.subtract))
                    link(nc.gpsimd.tensor_tensor(w(9), g[:, b, 1, :], g[:, b, 0, :], ALU.subtract))
                    slope(w(8), w(9))
                    move(q, 1)
                else:
                    miss(q, 2, 10)
                    link(nc.gpsimd.tensor_tensor(w(11), w(10), w(7), ALU.mult))
                    link(nc.gpsimd.tensor_scalar(w(11), w(11), 0.0, None, ALU.is_gt))
                    link(nc.gpsimd.tensor_tensor(w(8), w(8), w(11), ALU.mult))
                    link(nc.gpsimd.tensor_tensor(w(9), w(9), w(11), ALU.mult))
                    link(nc.gpsimd.tensor_tensor(w(8), nt[:, b, 1, :], w(8), ALU.subtract))
                    link(nc.gpsimd.tensor_tensor(w(9), g[:, b, 1, :], w(9), ALU.subtract))
                    link(nc.gpsimd.tensor_tensor(w(8), nt[:, b, 2, :], w(8), ALU.subtract))
                    link(nc.gpsimd.tensor_tensor(w(9), g[:, b, 2, :], w(9), ALU.subtract))
                    slope(w(8), w(9))
                    move(q, 2)

            def ranks(q):
                b = q % 2
                pool.wait_ge(counted, 4 * (q - FIRST) + 4)
                if q > FIRST + 1:
                    pool.wait_ge(probs_ready, 4 * (q - 1))
                link(nc.gpsimd.tensor_scalar(rank[:], cnt[:, b, :], -1.0, float(TOPK), ALU.mult, ALU.add))
                link(nc.gpsimd.tensor_scalar(y9[:, b, :, 0], nt[:, b, 3, :], -1.0, None, ALU.mult))
                rb = rank[:].rearrange("p (h o) -> p h o", o=1).to_broadcast([P, 4, 9])
                link(nc.gpsimd.tensor_tensor(hot[:, b, :, :], iota[:, :, :], rb, ALU.subtract))
                link(nc.gpsimd.tensor_scalar(hot[:, b, :, :], hot[:, b, :, :], 0.0, None, ALU.is_equal))
                link(nc.gpsimd.tensor_scalar(off[:], cnt[:, b, :], (LOW_C + HIGH_C) / 2, None, ALU.subtract))
                link(nc.gpsimd.tensor_tensor(off[:], off[:], off[:], ALU.mult))
                if q > FIRST:
                    pool.wait_ge(ring_full, RING["small", q + 1] + 1)
                nc.gpsimd.tensor_scalar(fail[:], off[:], ((HIGH_C - LOW_C) / 2) ** 2 + 0.5, None, ALU.is_gt)\
                    .then_inc(ranks_ready, 1)

            def keep_memory(n):
                q, nk = n // 4, n // 16 + 1
                pool.wait_ge(tp_taken, tcount(n))
                if q >= 2:
                    pool.wait_ge(ring_full, RING["out", q - 2] + 1)
                nc.gpsimd.tensor_copy(memPT[:, q % 2, n % 4, :], PT[0:MEM, n % 2, nk * P:(nk + 1) * P])\
                    .then_inc(mem_kept, 1)

            pool.wait_ge(consts_loaded, 16 * 7)
            for p in range(QUADS + 3):
                if needs_search(p - 1):
                    first_threshold(p - 1)
                if needs_search(p - 2):
                    ranks(p - 2)
                for h in range(4):
                    n = 4 * (p - 2) + h - 1
                    if h > 0 and needs_search(p - 1):
                        step(p - 1, h - 1)
                    if 0 <= n < 4 * QUADS:
                        keep_memory(n)
                if needs_search(p + 1):
                    start(p + 1)

        @block.scalar
        def _(act):
            for dst, src in ((ident[:], ident_d), (sel, sel_d.rearrange("k (c n) -> k c n", c=9)),
                             (cmask[:], cmask_d), (nz[:], nz_d), (kap[:], kap_d),
                             (iota[:, :, :], iota_d.rearrange("p (h k) -> p h k", h=4))):
                act.dma_start(dst, src).then_inc(consts_loaded, 16)
            act.dma_start(bob, bo.rearrange("(o n) -> o n", o=1).to_broadcast([P, D])).then_inc(consts_loaded, 16)
            act.dma_start(gateS[0:EXPERTS, :], gate_w).then_inc(ffn_loaded, 16)
            act.dma_start(gateS[EXPERTS:EXPERTS + 1, :], s_gw).then_inc(ffn_loaded, 16)
            act.dma_start(wg, w_gu[:, :, 0:FF].rearrange("e d f -> d e f")).then_inc(ffn_loaded, 16)
            act.dma_start(wu, w_gu[:, :, FF:2 * FF].rearrange("e d f -> d e f")).then_inc(ffn_loaded, 16)
            act.dma_start(wd, w_down.rearrange("(c t) f n -> (t f) c n", t=2)).then_inc(ffn_loaded, 16)
            for t, s in enumerate((s_gate, s_up)):
                for b, (a, n) in enumerate(SBLK):
                    act.dma_start(shS[0:n, t, b, :], s[a:a + n, :]).then_inc(ffn_loaded, 16)
            act.dma_start(sdS, s_down).then_inc(ffn_loaded, 16)
            act.wait_ge(var_ready, 1)
            nc.scalar.activation(st[:, 3, :], st[:, 2, :], ACT.Sqrt).then_inc(std_ready, 1)
            for i, (_, dst, rows, cols) in enumerate(blocks):
                act.wait_ge(tr_full, i + 1)
                nc.scalar.activation(dst, T[i % 3][0:rows, 0:cols], ACT.Copy).then_inc(tr_taken, 1)
            for t, dst in enumerate((M, PV)):
                act.wait_ge(scaled_used, NCH * (t + 1))
                nc.scalar.activation(dst[:, 0:PIECE], R[0][:, :], ACT.Copy).then_inc(prod_taken, 1)
            act.wait_ge(gexp_ready, 1)
            nc.scalar.activation(comb[:, :, :], lg[:, :, :], ACT.Exp).then_inc(gexp_done, 1)
            for i in range(4):
                act.wait_ge(ct_full, i + 1)
                nc.scalar.activation(combT[:, i * 512:(i + 1) * 512], T[i % 2][0:EXPERTS + 1, :], ACT.Copy)\
                    .then_inc(ct_taken, 1)
            for k in range(4 * NJ):
                m = SBLK[k % NJ - NPAIR][1] if k % NJ >= NPAIR else P
                act.wait_ge(gu_full, k + 1)
                if k >= 2:
                    act.wait_ge(h_ready, 2 * (k - 1))
                nc.scalar.activation(sg[0:m, k % 2, :], R[k % 2][0:m, 0:512], ACT.Silu).then_inc(gate_read, 1)

            k_sign = 0
            act.wait_ge(down_taken, 4)

            def exponent(n):
                q = n // 4
                wd_ = width(q)
                act.wait_ge(max_ready, q + 1)
                if n >= 3:
                    act.wait_ge(tp_full, tcount(n - 3))
                nc.scalar.activation(E[:, n % 3, 0:wd_], S[:, n % 8, 0:wd_], ACT.Exp,
                                     bias=mbias[:, q % 2, n % 4:n % 4 + 1], scale=UP).then_inc(exp_done, 1)

            def take_transposed(n):
                q = n // 4
                base = tcount(n) - len(tpieces(q))
                if n >= 2:
                    act.wait_ge(z_done, n - 1)
                    act.wait_ge(mem_kept, n - 1)
                for i, (a, b) in enumerate(tpieces(q)):
                    act.wait_ge(tp_full, base + i + 1)
                    nc.scalar.activation(PT[:, n % 2, a * P:b * P], T[(base + i) % 3][:, 0:(b - a) * P], ACT.Copy)\
                        .then_inc(tp_taken, 1)

            def take_z(q):
                act.wait_ge(z_done, 4 * (q + 1))
                if q >= 1:
                    act.wait_ge(ring_full, RING["out", q - 1] + 1)
                nc.scalar.activation(zst[:], Z[:, :], ACT.Copy).then_inc(z_taken, 1)

            def signs(q, s):
                nonlocal k_sign
                wd_ = width(q)
                act.wait_ge(step_ready, 4 * (q - FIRST) + s + 1)
                act.wait_ge(max_ready, q + 1)
                for h in range(4):
                    if k_sign >= 2:
                        act.wait_ge(signs_summed, k_sign - 1)
                    nc.scalar.activation(junk[:, k_sign % 2, 0:wd_], S[:, 4 * (q % 2) + h, 0:wd_], ACT.Sign,
                                         bias=nt[:, q % 2, s, h:h + 1],
                                         accum_out=g[:, q % 2, s, h:h + 1]).then_inc(signs_summed, 1)
                    k_sign += 1

            for p in range(QUADS + 3):
                for h in range(4):
                    n = 4 * (p - 2) + h
                    if 0 <= n < 4 * QUADS:
                        exponent(n)
                    if 1 <= n <= 4 * QUADS:
                        take_transposed(n - 1)
                    if h == 1 and 0 <= p - 3:
                        take_z(p - 3)
                    if h < 3 and needs_search(p - 1):
                        signs(p - 1, h)

        @block.vector
        def _(dve):
            chain = [0]

            def link(ins):
                chain[0] += 1
                ins.then_inc(dve_chain, 1)
                dve.wait_ge(dve_chain, chain[0])

            V = nc.vector

            def bc(ap, n):
                return ap.rearrange("p (k o) -> p k o", o=1).to_broadcast([ap.shape[0], ap.shape[1], n])

            dve.wait_ge(x_loaded, 16)
            link(V.tensor_reduce(st[:, 0, :], acc[:, :, :], AXX, ALU.add))
            link(V.tensor_scalar(st[:, 0, :], st[:, 0, :], 1.0 / D, None, ALU.mult))
            link(V.tensor_tensor(XN[:, :, :], acc[:, :, :], bc(st[:, 0, :], D), ALU.subtract))
            link(V.tensor_tensor(xsq, XN[:, :, :], XN[:, :, :], ALU.mult))
            link(V.tensor_reduce(st[:, 1, :], xsq, AXX, ALU.add))
            V.tensor_scalar(st[:, 2, :], st[:, 1, :], 1.0 / D, EPS, ALU.mult, ALU.add).then_inc(var_ready, 1)
            dve.wait_ge(std_ready, 1)
            link(V.reciprocal(st[:, 4, :], st[:, 3, :]))
            link(V.tensor_tensor(st[:, 5, :], st[:, 4, :], st[:, 4, :], ALU.mult))
            link(V.tensor_tensor(st[:, 5, :], st[:, 5, :], st[:, 2, :], ALU.mult))
            link(V.tensor_scalar(st[:, 5, :], st[:, 5, :], -0.5, 1.5, ALU.mult, ALU.add))
            link(V.tensor_tensor(st[:, 4, :], st[:, 4, :], st[:, 5, :], ALU.mult))
            V.tensor_tensor(XN[:, :, :], XN[:, :, :], bc(st[:, 4, :], D), ALU.mult).then_inc(xn_ready, 1)
            dve.wait_ge(consts_loaded, 16 * 7)
            V.tensor_copy(identb[:], ident[:]).then_inc(casts_done, 1)
            V.tensor_copy(cmaskb[:], cmask[:]).then_inc(casts_done, 1)
            bo_rep = bob.rearrange("p (o d) -> p o d", o=1).to_broadcast([P, NB, D])
            link(V.tensor_tensor(acc[:, :, :], acc[:, :, :], bo_rep, ALU.add))

            dve.wait_ge(mixB_full, 1)
            link(V.tensor_scalar(preB.rearrange("p c k -> p (c k)"), R[0][:, 0:P], DH ** -0.5 * DOWN, None, ALU.mult))
            link(V.tensor_copy(postB.rearrange("p c k -> p (c k)"), R[0][:, P:2 * P]))
            for t in range(2):
                B = preB if t == 0 else postB
                for c in range(NCH):
                    k = NCH * t + c
                    if k >= 2:
                        dve.wait_ge(scaled_used, k - 1)
                    src = wT[:, 1, c, :] if t == 0 else woS[:, c, :]
                    if t == 0:
                        dve.wait_ge(tr_taken, n_att_tr)
                        V.tensor_tensor(scaledm[:, k % 2, :, :], bc(B[:, c, :], MEM),
                                        memT[:, 0, c, :].rearrange("p (o m) -> p o m", o=1).to_broadcast([P, HEADS, MEM]),
                                        ALU.mult).then_inc(scaled_ready, 1)
                    else:
                        dve.wait_ge(att_loaded, 16 * 22)
                    V.tensor_tensor(scaled[:, k % 2, :, :], bc(B[:, c, :], D),
                                    src.rearrange("p (o n) -> p o n", o=1).to_broadcast([P, HEADS, D]),
                                    ALU.mult).then_inc(scaled_ready, 1)
                dve.wait_ge(scaled_used, NCH * (t + 1))
                if t == 0:
                    link(V.tensor_copy(M[:, PIECE:], R[1][:, :]))
                    link(V.tensor_copy(Kmem[:], T[0][:, 0:HEADS * MEM]))
                else:
                    link(V.tensor_copy(PV[:, PIECE:], R[1][:, :]))
                    for i in range(3):
                        link(V.tensor_copy(MV[:, i * 512:(i + 1) * 512], T[i][0:MEM, :]))
                    link(V.tensor_copy(MV[:, 1536:2048], Z[0:MEM, :]))
                dve.sem_inc(prod_taken, 1)

            dve.wait_ge(gates_full, 1)
            link(V.tensor_copy(lg[:, :, :], T[0][:, 0:NB * 17].rearrange("p (b e) -> p b e", b=NB)))
            dve.sem_inc(gates_taken, 1)
            lo16, down = lg[:, :, 0:EXPERTS], rt[:, 3, :, :]
            index = rt[:, 2, :, :]
            m1, m2 = st[:, 0, :], st[:, 1, :]
            for e in range(EXPERTS):
                link(V.memset(index[:, :, e:e + 1], float(EXPERTS - e)))
            for t, m in ((0, m1), (1, m2)):
                left = lo16 if t == 0 else down
                link(V.tensor_reduce(m, left, AXX, ALU.max))
                link(V.tensor_tensor(rt[:, t, :, :], left, bc(m, EXPERTS), ALU.is_equal))
                link(V.tensor_tensor(rt[:, t, :, :], rt[:, t, :, :], index, ALU.mult))
                link(V.tensor_reduce(st[:, 2, :], rt[:, t, :, :], AXX, ALU.max))
                link(V.tensor_tensor(rt[:, t, :, :], index, bc(st[:, 2, :], EXPERTS), ALU.is_equal))
                if t == 0:
                    link(V.scalar_tensor_tensor(out=down, in0=rt[:, 0, :, :], scalar=LOWEST, in1=lo16,
                                                op0=ALU.mult, op1=ALU.add))
            link(V.tensor_tensor(rt[:, 0, :, :], rt[:, 0, :, :], rt[:, 1, :, :], ALU.add))
            link(V.tensor_tensor(lo16, lo16, bc(m1, EXPERTS), ALU.subtract))
            V.tensor_scalar(lg[:, :, 16:17], lg[:, :, 16:17], -1.0, None, ALU.mult).then_inc(gexp_ready, 1)
            dve.wait_ge(gexp_done, 1)
            ce = comb[:, :, 0:EXPERTS]
            link(V.tensor_tensor(ce, ce, rt[:, 0, :, :], ALU.mult))
            link(V.tensor_reduce(st[:, 2, :], ce, AXX, ALU.add))
            link(V.reciprocal(st[:, 3, :], st[:, 2, :]))
            link(V.tensor_tensor(ce, ce, bc(st[:, 3, :], EXPERTS), ALU.mult))
            link(V.tensor_scalar(comb[:, :, 16:17], comb[:, :, 16:17], 1.0, None, ALU.add))
            V.reciprocal(comb[:, :, 16:17], comb[:, :, 16:17]).then_inc(comb_ready, 1)

            for c in range(4):
                for j in range(NJ):
                    k = NJ * c + j
                    m = SBLK[j - NPAIR][1] if j >= NPAIR else P
                    dve.wait_ge(gate_read, k + 1)
                    if c >= 1:
                        dve.wait_ge(down_full, c)
                    V.tensor_tensor(su[0:m, k % 2, :], sg[0:m, k % 2, :], R[k % 2][0:m, 512:1024], ALU.mult)\
                        .then_inc(h_ready, 1)
                    dve.wait_ge(h_ready, 2 * k + 1)
                    V.tensor_tensor(H[0:m, j, :], su[0:m, k % 2, :], T[k % 2][0:m, :], ALU.mult).then_inc(h_ready, 1)
                dve.wait_ge(down_full, c + 1)
                V.tensor_tensor(acc[:, 4 * c:4 * c + 4, :], acc[:, 4 * c:4 * c + 4, :],
                                Z[:, :].rearrange("p (b d) -> p b d", b=4), ALU.add).then_inc(down_taken, 1)
            dve.wait_ge(down_taken, 4)
            for i in range(3):
                V.memset(T[i][:, :], 0.0).then_inc(t_banks_zeroed, 1)

            def general(n, target, link_):
                wd_ = width(n // 4)
                src = S[:, n % 8, 0:wd_]
                for i in range(TOPK // 8):
                    link_(V.max(t8[:], src))
                    if i < TOPK // 8 - 1:
                        link_(V.match_replace(out=Y[:, 0:wd_], in_to_replace=t8[:], in_values=src, imm_value=LOWEST))
                        src = Y[:, 0:wd_]
                link_(V.tensor_copy(target, t8[:, 7:8]))

            def take_scores(n):
                q = n // 4
                if q >= 2:
                    dve.wait_ge(probs_ready, n - 7)
                for i, (a, b) in enumerate(pieces(q)):
                    k = RING["score", n, i]
                    dve.wait_ge(ring_full, k + 1)
                    V.tensor_scalar(S[:, n % 8, a:b], R[k % 2][:, 0:b - a], 1.0, LOWEST, ALU.mult, ALU.max,
                                    accum_out=mxp[:, n % 8, i:i + 1]).then_inc(ring_taken, 1)

            def maxima(q):
                b = q % 2
                np_ = len(pieces(q))
                dve.wait_ge(ring_taken, RING["score", 4 * q + 3, np_ - 1] + 1)
                if q >= 2:
                    dve.wait_ge(exp_done, 4 * (q - 1))
                link(V.tensor_reduce(mxq[:, b, :], mxp[:, 4 * b:4 * b + 4, 0:np_], AXX, ALU.max))
                V.tensor_scalar(mbias[:, b, :], mxq[:, b, :], -UP, None, ALU.mult).then_inc(max_ready, 1)

            def take_queries(q):
                k = RING["query", q]
                dve.wait_ge(ring_full, k + 1)
                if needs_search(q - 2):
                    dve.wait_ge(squares_ready, q - 2 - FIRST + 1)
                V.tensor_copy(QT[:, q % 2, :], R[k % 2][:, 0:512]).then_inc(ring_taken, 1)

            def take_small(p):
                k = RING["small", p]
                dve.wait_ge(ring_full, k + 1)
                if needs_search(p - 2):
                    link(V.tensor_copy(failed[:], R[k % 2][0:1, 512:517]))
                if needs_search(p):
                    if p >= FIRST + 2:
                        dve.wait_ge(step_ready, 4 * (p - 2 - FIRST) + 1)
                    link(V.tensor_copy(sg2[:, p % 2, :], R[k % 2][:, 0:4]))
                dve.sem_inc(ring_taken, 1)

            def repair(q):
                b = q % 2
                any_failed = dve.value_load(failed[0:1, 4:5], min_val=0, max_val=P * 4)
                with dve.If(any_failed > 0):
                    for h in range(4):
                        head_failed = dve.value_load(failed[0:1, h:h + 1], min_val=0, max_val=P)
                        with dve.If(head_failed > 0):
                            steps = [0]

                            def glink(ins):
                                steps[0] += 1
                                ins.then_inc(general_chain, 1)
                                dve.wait_ge(general_chain, steps[0])

                            general(4 * q + h, y9[:, b, h, 0:1], glink)
                            glink(V.memset(hot[:, b, h, :], 0.0))
                            glink(V.memset(hot[:, b, h, 0:1], 1.0))
                            dve.sem_clear(general_chain)

            def count(q):
                wd_ = width(q)
                b = q % 2
                dve.wait_ge(step_ready, 4 * (q - FIRST) + 4)
                for h in range(4):
                    n = 4 * q + h
                    if h == 0:
                        link(V.tensor_scalar(thr[:, 4 * b:4 * b + 4], nt[:, b, 3, :], -1.0, None, ALU.mult))
                    V.tensor_scalar(Y[:, 0:wd_], S[:, n % 8, 0:wd_], thr[:, n % 8:n % 8 + 1], 0.0,
                                    ALU.is_ge, ALU.add, accum_out=cnt[:, b, h:h + 1]).then_inc(counted, 1)
                    dve.wait_ge(counted, 4 * (q - FIRST) + h + 1)

            def below(n):
                q = n // 4
                wd_ = width(q)
                s = S[:, n % 8, 0:wd_]
                link(V.scalar_tensor_tensor(out=Y[:, 0:wd_], in0=s, scalar=thr[:, n % 8:n % 8 + 1], in1=s,
                                            op0=ALU.is_ge, op1=ALU.subtract, reverse1=True))
                link(V.max(y9[:, q % 2, n % 4, 1:9], Y[:, 0:wd_]))

            def choose(n):
                q = n // 4
                if n % 4 == 0:
                    dve.wait_ge(ranks_ready, q - FIRST + 1)
                link(V.scalar_tensor_tensor(out=pick[:], in0=y9[:, q % 2, n % 4, :], scalar=1.0,
                                            in1=hot[:, q % 2, n % 4, :], op0=ALU.mult, op1=ALU.mult,
                                            accum_out=thr[:, n % 8:n % 8 + 1]))

            def weights(n):
                wd_ = width(n // 4)
                dve.wait_ge(exp_done, n + 1)
                V.scalar_tensor_tensor(out=E[:, n % 3, 0:wd_], in0=S[:, n % 8, 0:wd_],
                                       scalar=thr[:, n % 8:n % 8 + 1], in1=E[:, n % 3, 0:wd_],
                                       op0=ALU.is_ge, op1=ALU.mult, accum_out=rsum[:, n % 8:n % 8 + 1])\
                    .then_inc(probs_ready, 1)

            def inverse(q):
                dve.wait_ge(probs_ready, 4 * (q + 1))
                link(V.reciprocal(rinv[:, q % 2, :], rsum[:, 4 * (q % 2):4 * (q % 2) + 4]))

            def add_out(q):
                k = RING["out", q]
                b = q // 4
                dve.wait_ge(ring_full, k + 1)
                for h in range(4):
                    ins = V.scalar_tensor_tensor(out=acc[:, b, :], in0=R[k % 2][:, h * D:(h + 1) * D],
                                                 scalar=rinv[:, q % 2, h:h + 1], in1=acc[:, b, :],
                                                 op0=ALU.mult, op1=ALU.add)
                    if h == 3:
                        ins.then_inc(ring_taken, 1)
                        dve.wait_ge(ring_taken, k + 1)
                        if q % 4 == 3:
                            dve.sem_inc(rows_ready, 1)
                    else:
                        link(ins)

            take_queries(0)
            for p in range(QUADS + 3):
                q = p - 2
                if needs_search(q):
                    count(q)
                for h in range(4):
                    n = 4 * q + h
                    if 0 <= q < QUADS:
                        if needs_search(q):
                            below(n)
                        else:
                            general(n, thr[:, n % 8:n % 8 + 1], link)
                    if h == 0 and ("small", p) in RING:
                        take_small(p)
                        if needs_search(q):
                            dve.wait_ge(ranks_ready, q - FIRST + 1)
                            repair(q)
                    if 0 <= q < QUADS:
                        if needs_search(q):
                            choose(n)
                        weights(n)
                    if h == 2 and 0 <= p - 3:
                        add_out(p - 3)
                    if p < QUADS:
                        take_scores(4 * p + h)
                    if h == 1 and p + 1 < QUADS:
                        take_queries(p + 1)
                if 0 <= q < QUADS:
                    inverse(q)
                if p < QUADS:
                    maxima(p)

        @block.tensor
        def _(pe):
            mm, tr = nc.tensor.matmul, nc.tensor.transpose

            pe.wait_ge(consts_loaded, 16 * 7)
            for i, (parts, _, _, _) in enumerate(blocks):
                if i == 0:
                    pe.wait_ge(att_loaded, 16 * 22)
                if i == n_att_tr:
                    pe.wait_ge(ffn_loaded, 16 * 12)
                if i == n_w_tr:
                    pe.wait_ge(xn_ready, 1)
                if i >= 3:
                    pe.wait_ge(tr_taken, i - 2)
                at = 0
                for src, rows, cols in parts:
                    last = tr(T[i % 3][0:cols, at:at + rows], src, ident[0:rows, 0:rows])
                    at += rows
                last.then_inc(tr_full, 1)
            pe.wait_ge(tr_taken, n_att_tr)
            for t, m in enumerate((preS, postT)):
                for c in range(NCH):
                    last = mm(R[0][:, t * P + c * 16:t * P + (c + 1) * 16], sel[0:HEADS, c, :], m, start=True, stop=True)
            last.then_inc(mixB_full, 1)
            pe.wait_ge(tr_taken, n_tr)
            ready = 0
            for t in range(2):
                if t == 1:
                    pe.wait_ge(prod_taken, 2)
                for c in range(NCH):
                    k = NCH * t + c
                    ready += 2 if t == 0 else 1
                    pe.wait_ge(scaled_ready, ready)
                    lhs = wT[:, 0, c, :] if t == 0 else wT[:, 2, c, :]
                    for i in range(4):
                        last = mm(R[i // 2][:, (i % 2) * 512:(i % 2 + 1) * 512], lhs,
                                  scaled[:, k % 2, 4 * i:4 * i + 4, :].rearrange("p k n -> p (k n)"),
                                  start=(c == 0), stop=(c == NCH - 1))
                    if t == 0:
                        last = mm(T[0][:, 0:HEADS * MEM], lhs, scaledm[:, k % 2, :, :].rearrange("p k m -> p (k m)"),
                                  start=(c == 0), stop=(c == NCH - 1))
                    else:
                        for i in range(4):
                            bank = T[i] if i < 3 else Z
                            last = mm(bank[0:MEM, :], memT[:, 1, c, :],
                                      scaled[:, k % 2, 4 * i:4 * i + 4, :].rearrange("p k n -> p (k n)"),
                                      start=(c == 0), stop=(c == NCH - 1))
                    last.then_inc(scaled_used, 1)
            pe.wait_ge(prod_taken, 4)
            for b in range(NB):
                last = mm(T[0][:, 17 * b:17 * (b + 1)], xnT[:, b * P:(b + 1) * P], gateT, start=True, stop=True)
            last.then_inc(gates_full, 1)
            pe.wait_ge(comb_ready, 1)
            pe.wait_ge(gates_taken, 1)
            for i in range(4):
                if i >= 2:
                    pe.wait_ge(ct_taken, i - 1)
                for b in range(4):
                    last = tr(T[i % 2][0:17, b * P:(b + 1) * P], comb[:, 4 * i + b, :], ident[:, :])
                last.then_inc(ct_full, 1)
            pe.wait_ge(ct_taken, 4)
            for c in range(4):
                cols = xnT[:, c * 512:(c + 1) * 512]
                for j in range(NJ):
                    k = NJ * c + j
                    if j < NPAIR:
                        m = P
                        lg_, lu_ = (a[:, 2 * j:2 * j + 2, :].rearrange("p e f -> p (e f)") for a in (wg, wu))
                        ls_ = sel[0:17, j, :]
                    else:
                        a0, m = SBLK[j - NPAIR]
                        lg_, lu_ = (shT[:, t, j - NPAIR, 0:m] for t in range(2))
                        ls_ = sel[0:17, NPAIR, 0:m]
                    if k >= 2:
                        pe.wait_ge(h_ready, 2 * (k - 1))
                    mm(R[k % 2][0:m, 0:512], lg_, cols, start=True, stop=True)
                    mm(R[k % 2][0:m, 512:1024], lu_, cols, start=True, stop=True)
                    mm(T[k % 2][0:m, :], ls_, combT[:, c * 512:(c + 1) * 512], start=True, stop=True)\
                        .then_inc(gu_full, 1)
                pe.wait_ge(h_ready, 2 * NJ * (c + 1))
                if c >= 1:
                    pe.wait_ge(down_taken, c)
                for b in range(4):
                    for j in range(NJ):
                        m = SBLK[j - NPAIR][1] if j >= NPAIR else P
                        rhs = wd[:, j, :] if j < NPAIR else sdT[0:m, j - NPAIR, :]
                        last = mm(Z[:, b * D:(b + 1) * D], H[0:m, j, b * P:(b + 1) * P], rhs,
                                  start=(j == 0), stop=(j == NJ - 1))
                last.then_inc(down_full, 1)

            pe.wait_ge(down_taken, 4)
            pe.wait_ge(t_banks_zeroed, 3)
            pe.wait_ge(casts_done, 2)
            pe.wait_ge(ones_set, 1)

            def slot(item):
                k = RING[item]
                if k >= 2:
                    pe.wait_ge(ring_taken, k - 1)
                return R[k % 2]

            def queries(q):
                r, ps = q // 4, slot(("query", q))
                for h in range(4):
                    k = 4 * (q % 4) + h
                    last = mm(ps[:, h * P:(h + 1) * P], M[:, k * D:(k + 1) * D], xnT[:, r * P:(r + 1) * P],
                              start=True, stop=True)
                last.then_inc(ring_full, 1)

            def small(p):
                ps = slot(("small", p))
                if needs_search(p):
                    pe.wait_ge(squares_ready, p - FIRST + 1)
                    for h in range(4):
                        last = mm(ps[:, h:h + 1], sq[:, h * P:(h + 1) * P], ones[:, 0:1], start=True, stop=True)
                if needs_search(p - 2):
                    pe.wait_ge(ranks_ready, p - 2 - FIRST + 1)
                    mm(ps[0:1, 512:516], ones[:, 0:1], fail[:, :], start=True, stop=True)
                    for h in range(4):
                        last = mm(ps[0:1, 516:517], ones[:, 0:1], fail[:, h:h + 1], start=(h == 0), stop=(h == 3))
                last.then_inc(ring_full, 1)

            def scores(n):
                q, r, h = n // 4, n // 16, n % 4
                keys = P * (r + 1)
                if h == 0:
                    pe.wait_ge(ring_taken, RING["query", q] + 1)
                for i, (a, b) in enumerate(pieces(q)):
                    ps = slot(("score", n, i))
                    for s in range(a, b, 512):
                        e = min(s + 512, b)
                        ek = min(e, keys)
                        if ek > s:
                            diag = s <= r * P < ek
                            last = mm(ps[:, s - a:ek - a], QT[:, q % 2, h * P:(h + 1) * P], xnT[:, s:ek],
                                      start=True, stop=not diag)
                            if diag:
                                last = mm(ps[:, r * P - a:keys - a], identb[:], cmaskb[:], start=False, stop=True)
                        if e > keys:
                            k = n % 16
                            last = mm(ps[:, keys - a:e - a], xnT[:, r * P:(r + 1) * P], Kmem[:, k * MEM:(k + 1) * MEM],
                                      start=True, stop=True)
                    last.then_inc(ring_full, 1)

            def transposes(n):
                q = n // 4
                nk = q // 4 + 1
                base = tcount(n) - len(tpieces(q))
                pe.wait_ge(probs_ready, n + 1)
                for i, (a, b) in enumerate(tpieces(q)):
                    if base + i >= 3:
                        pe.wait_ge(tp_taken, base + i - 2)
                    for j in range(a, b):
                        cols = P if j < nk else MEM
                        last = tr(T[(base + i) % 3][0:cols, (j - a) * P:(j - a + 1) * P],
                                  E[:, n % 3, j * P:j * P + cols], ident[:])
                    last.then_inc(tp_full, 1)

            def values(n):
                q, h = n // 4, n % 4
                nk = q // 4 + 1
                if h == 0 and q >= 1:
                    pe.wait_ge(z_taken, q)
                pe.wait_ge(tp_taken, tcount(n))
                for j in range(nk):
                    last = mm(Z[:, h * P:(h + 1) * P], XN[:, j, :], PT[:, n % 2, j * P:(j + 1) * P],
                              start=(j == 0), stop=(j == nk - 1))
                last.then_inc(z_done, 1)

            def project(q):
                ps = slot(("out", q))
                pe.wait_ge(z_taken, q + 1)
                pe.wait_ge(mem_kept, 4 * (q + 1))
                for h in range(4):
                    k = 4 * (q % 4) + h
                    mm(ps[:, h * D:(h + 1) * D], zst[:, h * P:(h + 1) * P], PV[:, k * D:(k + 1) * D],
                       start=True, stop=False)
                    last = mm(ps[:, h * D:(h + 1) * D], memPT[:, q % 2, h, :], MV[:, k * D:(k + 1) * D],
                              start=False, stop=True)
                last.then_inc(ring_full, 1)

            queries(0)
            for p in range(QUADS + 3):
                if ("small", p) in RING:
                    small(p)
                for h in range(4):
                    n = 4 * (p - 2) + h
                    if h == 2 and 0 <= p - 3:
                        project(p - 3)
                    if p < QUADS:
                        scores(4 * p + h)
                    if h == 1 and p + 1 < QUADS:
                        queries(p + 1)
                    if 0 <= n < 4 * QUADS:
                        transposes(n)
                    if 1 <= n <= 4 * QUADS:
                        values(n - 1)


_INS = ["L0_attn_x", "L0_attn_Wq", "L0_attn_Wk", "L0_attn_Wv", "L0_attn_pre_proj", "L0_attn_post_proj",
        "L0_attn_mem_k", "L0_attn_mem_v", "L0_attn_Wo", "L0_attn_bo", "L0_ffn_gate_w", "L0_ffn_w_gate_up",
        "L0_ffn_w_down", "L0_ffn_shared_w_gate", "L0_ffn_shared_w_up", "L0_ffn_shared_w_down",
        "L0_ffn_shared_gate_w"]


def shape_tables():
    import numpy as np

    def over(z):
        return 0.5 * math.erfc(z / math.sqrt(2.0))

    def density(z):
        return math.exp(-z * z / 2) / math.sqrt(2 * math.pi)

    sel = np.zeros((EXPERTS + 1, 9, P), np.float32)
    for c in range(8):
        for p in range(P):
            sel[2 * c + p // DH, c, p] = 1.0
    sel[EXPERTS, 8, :] = 1.0
    i = np.arange(P)
    cmask = np.where(i[None, :] > i[:, None], np.float32(MASKED), np.float32(0.0)).astype(np.float32)
    spread = 4.6
    z = np.zeros(N)
    kap = np.ones(N)
    for r in range(P, N):
        lo, hi = -2.0, 5.0
        for _ in range(40):
            mid = (lo + hi) / 2
            above = (r + 1) * over(mid) + MEM * over(mid / spread)
            lo, hi = (mid, hi) if above > AIM else (lo, mid)
        z[r] = mid
        kap[r] = 0.5 / ((r + 1) * density(mid) + MEM * density(mid / spread) / spread)
    return {"ident": np.eye(P, dtype=np.float32), "sel": sel.reshape(EXPERTS + 1, 9 * P), "cmask": cmask,
            "nz": np.ascontiguousarray(-z.reshape(NB, P).T).astype(np.float32),
            "kap": np.ascontiguousarray(kap.reshape(NB, P).T).astype(np.float32),
            "iota": np.tile(np.arange(9, dtype=np.float32), (P, 4))}


def kernel(**inputs):
    import numpy as np
    import concourse.bacc as bacc
    from concourse.bass_utils import run_bass_kernel_spmd

    nc = bacc.Bacc("TRN2", target_bir_lowering=False, num_devices=1)
    arrays = {f"in_{n}": np.ascontiguousarray(inputs[n]) for n in _INS}
    arrays["in_L0_attn_x"] = arrays["in_L0_attn_x"].reshape(N, D)
    arrays.update({f"tab_{k}": v for k, v in shape_tables().items()})
    args = [nc.dram_tensor(k, v.shape, mybir.dt.from_np(v.dtype), kind="ExternalInput").ap()
            for k, v in arrays.items()]
    out = nc.dram_tensor("out_y", (N, D), F32, kind="ExternalOutput").ap()
    build(nc, *args, out)
    r = run_bass_kernel_spmd(nc, [arrays], core_ids=[0])
    return r.results[0]["out_y"].reshape(1, N, D)
```

```python
import math
from contextlib import ExitStack

import concourse.bass as bass
from concourse import mybir

F32 = mybir.dt.float32
BF16 = mybir.dt.bfloat16
I32 = mybir.dt.int32
ALU = mybir.AluOpType
ACT = mybir.ActivationFunctionType
AXX = mybir.AxisListType.X

N = 2048
D = 128
P = 128
NB = N // P
HEADS = 16
DH = 64
MEM = 16
TOPK = 64
NCH = HEADS * DH // P
INNER = HEADS * DH
EXPERTS = 16
FF = 64
SHARED = 352
NPAIR = EXPERTS // 2
SBLK = [(0, 128), (128, 128), (256, 96)]
NJ = NPAIR + len(SBLK)
EPS = 1e-5
SCALE_BITS = 40
DOWN = 2.0 ** -SCALE_BITS
UP = 2.0 ** SCALE_BITS
MASKED = -(2.0 ** 40)
LOWEST = -3.0e38
QUADS = NB * 4
WMAX = N + MEM
PIECE = 1024
NBLK = NB + 1
FIRST = 4
AIM = 60.2
NEAR = 4.1
ROUNDS = 4
NUDGE = 1.0 - 2.0 ** -24
NEXT = 0.75 * 2.0 ** -23


def width(q):
    return P * (q // 4 + 1) + MEM


def pieces(q):
    w = width(q)
    return [(a, min(a + PIECE, w)) for a in range(0, w, PIECE)]


def tpieces(q):
    nb = q // 4 + 2
    return [(a, min(a + 4, nb)) for a in range(0, nb, 4)]


def ring_items():
    items = []
    for p in range(-1, QUADS + 3):
        if p == -1:
            items.append(("query", 0))
            continue
        if needs_search(p) or needs_search(p - 2):
            items.append(("small", p))
        for h in range(4):
            if h == 2 and p + 1 < QUADS:
                items.append(("query", p + 1))
            if h == 3 and 0 <= p - 3 < QUADS:
                items.append(("out", p - 3))
            if p < QUADS:
                items += [("score", 4 * p + h, i) for i in range(len(pieces(p)))]
    return items


def needs_search(q):
    return FIRST <= q < QUADS


RING = {item: i for i, item in enumerate(ring_items())}


def tcount(n):
    return sum(4 * len(tpieces(q)) for q in range(n // 4)) + (n % 4 + 1) * len(tpieces(n // 4))


def build(nc, x, wq, wk, wv, pre, post, mem_k, mem_v, wo, bo, gate_w, w_gu, w_down, s_gate, s_up, s_down,
          s_gw, ident_d, sel_d, cmask_d, nz_d, kap_d, iota_d, out):
    ctx = ExitStack()
    with ctx:
        def sb(name, shape, dt=F32):
            return ctx.enter_context(nc.sbuf_tensor(name, shape, dt))

        def sem(name):
            return ctx.enter_context(nc.semaphore(name))

        S = sb("S", [P, 8, WMAX])
        E = sb("E", [P, 3, WMAX])
        Y = sb("Y", [P, WMAX])
        junk = sb("junk", [P, 2, WMAX], BF16)
        PT = sb("PT", [P, 2, NBLK * P])
        xnT = sb("xnT", [P, N])
        XN = sb("XN", [P, NB, D])
        M = sb("M", [P, HEADS * D])
        PV = sb("PV", [P, HEADS * D])
        MV = sb("MV", [MEM, HEADS * D])
        Kmem = sb("Kmem", [P, HEADS * MEM])
        acc = sb("acc", [P, NB, D])
        QT = sb("QT", [P, 2, 4 * P])
        sq = sb("sq", [P, 4 * P])
        zst = sb("zst", [P, 4 * P])
        ident = sb("ident", [P, P])
        identb = sb("identb", [P, P], BF16)
        cmask = sb("cmask", [P, P])
        cmaskb = sb("cmaskb", [P, P], BF16)
        ones = sb("ones", [P, 1])
        iota = sb("iota", [P, 4, 17])
        powers = sb("powers", [P, 2, 4])
        centres = sb("centres", [P, 2, 4])
        nz = sb("nz", [P, NB])
        kap = sb("kap", [P, NB])
        mxp = sb("mxp", [P, 8, 3])
        mxq = sb("mxq", [P, 2, 4])
        mbias = sb("mbias", [P, 2, 4])
        sg2 = sb("sg2", [P, 2, 4])
        tg = sb("tg", [P, 2, ROUNDS, 2, 4])
        diff = sb("diff", [P, 2, 2, 4])
        slope = sb("slope", [P, 2, 4])
        prior = sb("prior", [P, 2, 2, 4])
        far = sb("far", [P, 2, 4])
        inverse_ = sb("inverse_", [P, 4])
        away = sb("away", [P, 4])
        negative = sb("negative", [P, 4])
        shift = sb("shift", [P, 4])
        tiny = sb("tiny", [P, 2, 4])
        mark = sb("mark", [P, 2, 4])
        sigma = sb("sigma", [P, 4])
        miss = sb("miss", [P, 3, 4])
        move = sb("move", [P, 4])
        raw = sb("raw", [P, 3, 4])
        rank = sb("rank", [P, 4])
        off = sb("off", [P, 2, 4])
        hot = sb("hot", [P, 2, 4, 17])
        fail = sb("fail", [P, 8])
        failed = sb("failed", [1, 9], I32)
        y17 = sb("y17", [P, 2, 4, 17])
        t8 = sb("t8", [P, 8])
        pick = sb("pick", [P, 2, 17])
        thr = sb("thr", [P, 8])
        rsum = sb("rsum", [P, 8])
        rinv = sb("rinv", [P, 2, 4])
        memPT = sb("memPT", [MEM, 2, 4, P])
        st = sb("st", [P, 8, NB])

        Sf = S[:, :, :].rearrange("p a b -> p (a b)")
        Ef = E[:, :, :].rearrange("p a b -> p (a b)")
        PTf = PT[:, :, :].rearrange("p a b -> p (a b)")
        wqkv = Sf[:, 0:3 * INNER].rearrange("p (t n) -> p t n", t=3)
        wT = Sf[:, 3072:3072 + 3 * INNER].rearrange("p (t c n) -> p t c n", t=3, c=NCH)
        woS = Sf[:, 6144:7168].rearrange("p (c n) -> p c n", c=NCH)
        memS = Sf[:, 7168:7424].rearrange("p (t n) -> p t n", t=2)
        memT = Sf[:, 7424:7680].rearrange("p (t c m) -> p t c m", t=2, c=NCH)
        preB = Sf[:, 7680:7808].rearrange("p (c k) -> p c k", c=NCH)
        postB = Sf[:, 7808:7936].rearrange("p (c k) -> p c k", c=NCH)
        preS = Sf[0:HEADS, 7936:7952]
        postS = Sf[0:HEADS, 7952:7968]
        postT = Sf[0:HEADS, 7968:7984]
        gateS = Sf[0:EXPERTS + 1, 7984:8112]
        gateT = Sf[:, 8112:8129]
        sel = Sf[0:EXPERTS + 1, 8192:8192 + 9 * P].rearrange("p (c n) -> p c n", c=9)
        wg = Sf[:, 9344:10368].rearrange("p (e f) -> p e f", e=EXPERTS)
        wu = Sf[:, 10368:11392].rearrange("p (e f) -> p e f", e=EXPERTS)
        wd = Sf[:, 11392:12416].rearrange("p (c n) -> p c n", c=NPAIR)
        shS = Sf[:, 12416:12416 + 6 * P].rearrange("p (t b n) -> p t b n", t=2, b=3)
        shT = Sf[:, 13184:13184 + 6 * P].rearrange("p (t b n) -> p t b n", t=2, b=3)
        sdS = Sf[:, 13952:13952 + SHARED]
        sdT = Sf[:, 14304:14304 + 3 * P].rearrange("p (b n) -> p b n", b=3)
        lg = Sf[:, 14688:14688 + NB * 17].rearrange("p (b e) -> p b e", b=NB)
        comb = Sf[:, 14960:14960 + NB * 17].rearrange("p (b e) -> p b e", b=NB)
        rt = Sf[:, 15232:15232 + 4 * NB * EXPERTS].rearrange("p (t b e) -> p t b e", t=4, b=NB)
        scaled = Ef[:, 0:4096].rearrange("p (t k n) -> p t k n", t=2, k=HEADS)
        scaledm = Ef[:, 4096:4608].rearrange("p (t k m) -> p t k m", t=2, k=HEADS)
        bob = Ef[:, 4608:4736]
        H = Ef[:, 0:5632].rearrange("p (j n) -> p j n", j=NJ)
        sg = PTf[:, 0:1024].rearrange("p (t n) -> p t n", t=2)
        su = PTf[:, 1024:2048].rearrange("p (t n) -> p t n", t=2)
        combT = Y[0:EXPERTS + 1, 0:N]
        xsq = PTf[:, 2048:4096].rearrange("p (b d) -> p b d", b=NB)

        R = [ctx.enter_context(nc.psum_tensor(f"R{i}", [P, PIECE], F32)) for i in range(2)]
        T = [ctx.enter_context(nc.psum_tensor(f"T{i}", [P, 512], F32)) for i in range(3)]
        Z = ctx.enter_context(nc.psum_tensor("Z", [P, 512], F32))

        x_loaded, consts_loaded, att_loaded, ffn_loaded = (sem(s) for s in (
            "x_loaded", "consts_loaded", "att_loaded", "ffn_loaded"))
        ones_set = sem("ones_set")
        casts_done = sem("casts_done")
        var_ready = sem("var_ready")
        std_ready = sem("std_ready")
        xn_ready = sem("xn_ready")
        tr_full, tr_taken = sem("tr_full"), sem("tr_taken")
        mixB_full, mixB_taken = sem("mixB_full"), sem("mixB_taken")
        scaled_ready, scaled_used = sem("scaled_ready"), sem("scaled_used")
        prod_taken = sem("prod_taken")
        gates_full, comb_ready = sem("gates_full"), sem("comb_ready")
        gates_taken = sem("gates_taken")
        gexp_ready, gexp_done = sem("gexp_ready"), sem("gexp_done")
        ct_full, ct_taken = sem("ct_full"), sem("ct_taken")
        gu_full, gate_read, h_ready = sem("gu_full"), sem("gate_read"), sem("h_ready")
        down_full, down_taken = sem("down_full"), sem("down_taken")
        dve_chain, pool_chain = sem("dve_chain"), sem("pool_chain")
        t_banks_zeroed = sem("t_banks_zeroed")

        ring_full, ring_taken = sem("ring_full"), sem("ring_taken")
        tp_full, tp_taken = sem("tp_full"), sem("tp_taken")
        z_done, z_taken = sem("z_done"), sem("z_taken")
        exp_done = sem("exp_done")
        signs_summed = sem("signs_summed")
        squares_ready = sem("squares_ready")
        first_ready, step_ready = sem("first_ready"), sem("step_ready")
        squares_taken, marks_set = sem("squares_taken"), sem("marks_set")
        lowered, largest_found, chosen = sem("lowered"), sem("largest_found"), sem("chosen")
        inverted, added = sem("inverted"), sem("added")
        ranks_ready, fails_ready = sem("ranks_ready"), sem("fails_ready")
        max_ready = sem("max_ready")
        probs_ready = sem("probs_ready")
        rows_ready = sem("rows_ready")
        general_chain = sem("general_chain")
        stored = sem("stored")
        mem_kept = sem("mem_kept")

        blocks = []
        for t in range(3):
            for c0 in range(0, NCH, 4):
                blocks.append(([(wqkv[:, t, (c0 + i) * P:(c0 + i + 1) * P], P, P) for i in range(4)],
                               wT[:, t, c0:c0 + 4, :].rearrange("p c n -> p (c n)"), P, 512))
        blocks.append(([(memS[:, t, :], P, P) for t in range(2)],
                       memT[:, :, :, :].rearrange("p t c m -> p (t c m)"), P, 256))
        blocks.append(([(postS, HEADS, HEADS)], postT, HEADS, HEADS))
        n_att_tr = len(blocks)
        blocks.append(([(gateS, EXPERTS + 1, P)], gateT, P, EXPERTS + 1))
        for t in range(2):
            blocks.append(([(shS[0:n, t, b, :], n, P) for b, (_, n) in enumerate(SBLK)],
                           shT[:, t, :, :].rearrange("p b n -> p (b n)")[:, 0:SHARED], P, SHARED))
        for b, (a, n) in enumerate(SBLK):
            blocks.append(([(sdS[:, a:a + n], P, n)], sdT[0:n, b, :], n, P))
        n_w_tr = len(blocks)
        for b in range(0, NB, 4):
            blocks.append(([(XN[:, b + i, :], P, P) for i in range(4)], xnT[:, b * P:(b + 4) * P], P, 512))
        n_tr = len(blocks)

        block = ctx.enter_context(nc.Block())

        @block.sync
        def _(sp):
            sp.dma_start(acc[:, :, :], x.rearrange("(b p) d -> p b d", p=P)).then_inc(x_loaded, 16)
            for t, w in enumerate((wq, wk, wv)):
                sp.dma_start(wqkv[:, t, :], w).then_inc(att_loaded, 16)
            sp.dma_start(woS, wo.rearrange("(c p) n -> p c n", p=P)).then_inc(att_loaded, 16)
            sp.dma_start(preS, pre).then_inc(att_loaded, 16)
            sp.dma_start(postS, post).then_inc(att_loaded, 16)
            for t, m in enumerate((mem_k, mem_v)):
                for c in range(NCH):
                    sp.dma_start(memS[c * MEM:(c + 1) * MEM, t, :].rearrange("m (t e) -> m t e", t=2),
                                 m[2 * c:2 * c + 2].rearrange("t m e -> m t e")).then_inc(att_loaded, 16)
            for b in range(NB):
                sp.wait_ge(rows_ready, b + 1)
                sp.dma_start(out[b * P:(b + 1) * P, :], acc[:, b, :]).then_inc(stored, 16)
            sp.wait_ge(stored, 16 * NB)

        @block.gpsimd
        def _(pool):
            chain = [0]

            def link(ins):
                chain[0] += 1
                ins.then_inc(pool_chain, 1)
                pool.wait_ge(pool_chain, chain[0])

            nc.gpsimd.memset(ones[:], 1.0).then_inc(ones_set, 1)
            nc.gpsimd.memset(powers[:, 0, :], 0.5).then_inc(ones_set, 1)
            nc.gpsimd.memset(powers[:, 1, :], -1.0).then_inc(ones_set, 1)
            nc.gpsimd.memset(centres[:, 0, :], 4.0).then_inc(ones_set, 1)
            nc.gpsimd.memset(centres[:, 1, :], 8.0).then_inc(ones_set, 1)
            nc.gpsimd.memset(prior[:, 0, 1, :], 1.0).then_inc(ones_set, 1)
            nc.gpsimd.memset(prior[:, 1, 1, :], 1.0).then_inc(ones_set, 1)
            pool.wait_ge(ones_set, 7)

            def k_step(q, s):
                return (ROUNDS - 1) * (q - FIRST) + s

            def start(q):
                pool.wait_ge(ring_taken, RING["query", q] + 1)
                if q > FIRST:
                    pool.wait_ge(ring_full, RING["small", q - 1] + 1)
                nc.gpsimd.tensor_tensor(sq[:], QT[:, q % 2, :], QT[:, q % 2, :], ALU.mult).then_inc(squares_ready, 1)

            G = nc.gpsimd

            def first_threshold(q):
                b, r = q % 2, q // 4
                pool.wait_ge(ring_taken, RING["small", q] + 1)
                link(G.tensor_tensor(sigma[:], sg2[:, b, :], powers[:, 0, :], ALU.pow))
                link(G.tensor_scalar(prior[:, b, 0, :], sigma[:], kap[:, r:r + 1], None, ALU.mult))
                G.tensor_scalar(tg[:, b, 0, 0, :], sigma[:], nz[:, r:r + 1], None, ALU.mult).then_inc(first_ready, 1)
                pool.wait_ge(first_ready, q - FIRST + 1)

            def step(q, s):
                b = q % 2
                pool.wait_ge(signs_summed, 4 * (ROUNDS * (q - FIRST) + s + 1))
                link(G.tensor_scalar(miss[:, s, :], tg[:, b, s, 1, :], float(2 * AIM - width(q)), None, ALU.subtract))
                first = 1 if s < 2 else 0
                both = miss[:, s:s + 1, :].to_broadcast([P, 2 - first, 4])
                with_ = miss[:, s - 1 + first:s + 1, :]
                link(G.tensor_tensor(far[:, first:2, :], with_, both, ALU.mult))
                link(G.tensor_scalar(far[:, first:2, :], far[:, first:2, :], (2 * NEAR) ** 2, None, ALU.is_gt))
                link(G.tensor_tensor(move[:], far[:, 1, :], miss[:, s, :], ALU.mult))
                if s == 0:
                    m = prior[:, b, 0, :]
                else:
                    d = diff[:, s - 1, :, :]
                    link(G.tensor_tensor(d, tg[:, b, s, :, :], tg[:, b, s - 1, :, :], ALU.subtract))
                    if s == 2:
                        same = far[:, 0:1, :].to_broadcast([P, 2, 4])
                        link(G.tensor_tensor(diff[:, 0, :, :], diff[:, 0, :, :], same, ALU.mult))
                        link(G.tensor_tensor(d, d, diff[:, 0, :, :], ALU.add))
                    link(G.tensor_tensor(slope[:, :, :], d, d[:, 1:2, :].to_broadcast([P, 2, 4]), ALU.mult))
                    link(G.tensor_tensor(slope[:, :, :], slope[:, :, :], prior[:, b, :, :], ALU.add))
                    link(G.tensor_tensor(inverse_[:], slope[:, 1, :], powers[:, 1, :], ALU.pow))
                    link(G.tensor_tensor(slope[:, 0, :], slope[:, 0, :], inverse_[:], ALU.mult))
                    m = slope[:, 0, :]
                link(G.tensor_tensor(move[:], move[:], m, ALU.mult))
                if s < ROUNDS - 2:
                    G.tensor_tensor(tg[:, b, s + 1, 0, :], tg[:, b, s, 0, :], move[:], ALU.subtract)\
                        .then_inc(step_ready, 1)
                else:
                    link(G.tensor_tensor(raw[:, 0, :], tg[:, b, s, 0, :], move[:], ALU.subtract))
                    link(G.tensor_scalar(raw[:, 1, :], raw[:, 0, :], 3.0, None, ALU.mult))
                    link(G.tensor_tensor(raw[:, 2, :], raw[:, 1, :], raw[:, 0, :], ALU.subtract))
                    G.tensor_tensor(tg[:, b, s + 1, 0, :], raw[:, 1, :], raw[:, 2, :], ALU.subtract)\
                        .then_inc(step_ready, 1)
                pool.wait_ge(step_ready, k_step(q, s + 1))

            def marks(q):
                b = q % 2
                nt = tg[:, b, ROUNDS - 1, 0, :]
                if q > FIRST + 1:
                    pool.wait_ge(probs_ready, 4 * (q - 1))
                link(G.tensor_scalar(away[:], nt, -NEXT, None, ALU.mult))
                link(G.tensor_scalar(negative[:], nt, 0.0, None, ALU.is_gt))
                link(G.tensor_tensor(raw[:, 0, :], negative[:], away[:], ALU.mult))
                link(G.tensor_tensor(raw[:, 1, :], away[:], nt, ALU.subtract))
                G.tensor_tensor(y17[:, b, :, 0], raw[:, 1, :], raw[:, 0, :], ALU.subtract).then_inc(marks_set, 1)
                G.tensor_tensor(mark[:, b, :], raw[:, 0, :], nt, ALU.subtract).then_inc(marks_set, 1)
                link(G.tensor_scalar(shift[:], negative[:], 0.5, TOPK - width(q) / 2 - 0.25, ALU.mult, ALU.add))
                link(G.tensor_tensor(raw[:, 2, :], nt, nt, ALU.mult))
                for i in range(2):
                    link(G.tensor_scalar(tiny[:, i, :], raw[:, 2, :], 1e-36, None, ALU.is_lt))

            def ranks(q):
                b = q % 2
                pool.wait_ge(signs_summed, 4 * ROUNDS * (q - FIRST + 1))
                link(G.tensor_scalar(rank[:], tg[:, b, ROUNDS - 1, 1, :], -0.5, None, ALU.mult))
                link(G.tensor_tensor(rank[:], rank[:], shift[:], ALU.add))
                twice = rank[:].rearrange("p (o h) -> p o h", o=1).to_broadcast([P, 2, 4])
                link(G.tensor_tensor(off[:, :, :], twice, centres[:, :, :], ALU.subtract))
                link(G.tensor_tensor(off[:, :, :], off[:, :, :], off[:, :, :], ALU.mult))
                link(G.tensor_scalar(off[:, 0, :], off[:, 0, :], 4.5 ** 2, None, ALU.is_gt))
                link(G.tensor_scalar(off[:, 1, :], off[:, 1, :], 8.5 ** 2, None, ALU.is_gt))
                if q > FIRST:
                    pool.wait_ge(ring_full, RING["small", q + 1] + 1)
                G.tensor_tensor(fail[:].rearrange("p (i h) -> p i h", i=2), off[:, :, :], tiny[:, :, :], ALU.add)\
                    .then_inc(fails_ready, 1)
                rb = rank[:].rearrange("p (h o) -> p h o", o=1).to_broadcast([P, 4, 17])
                link(G.tensor_tensor(hot[:, b, :, :], iota[:, :, :], rb, ALU.subtract))
                link(G.tensor_tensor(hot[:, b, :, :], hot[:, b, :, :], hot[:, b, :, :], ALU.mult))
                G.tensor_scalar(hot[:, b, :, :], hot[:, b, :, :], 0.25, None, ALU.is_lt).then_inc(ranks_ready, 1)
                pool.wait_ge(fails_ready, q - FIRST + 1)
                pool.wait_ge(ranks_ready, q - FIRST + 1)

            def keep_memory(n):
                q, nk = n // 4, n // 16 + 1
                pool.wait_ge(tp_taken, tcount(n))
                if q >= 2:
                    pool.wait_ge(ring_full, RING["out", q - 2] + 1)
                nc.gpsimd.tensor_copy(memPT[:, q % 2, n % 4, :], PT[0:MEM, n % 2, nk * P:(nk + 1) * P])\
                    .then_inc(mem_kept, 1)

            pool.wait_ge(consts_loaded, 16 * 7)
            for p in range(QUADS + 3):
                if needs_search(p - 2):
                    ranks(p - 2)
                for h in range(4):
                    n = 4 * (p - 2) + h - 1
                    if 0 <= n < 4 * QUADS:
                        keep_memory(n)
                    if h < ROUNDS - 1 and needs_search(p - 1):
                        step(p - 1, h)
                        if h == ROUNDS - 2:
                            marks(p - 1)
                    if h == 1 and needs_search(p):
                        first_threshold(p)
                if needs_search(p + 1):
                    start(p + 1)

        @block.scalar
        def _(act):
            for dst, src in ((ident[:], ident_d), (sel, sel_d.rearrange("k (c n) -> k c n", c=9)),
                             (cmask[:], cmask_d), (nz[:], nz_d), (kap[:], kap_d),
                             (iota[:, :, :], iota_d.rearrange("p (h k) -> p h k", h=4))):
                act.dma_start(dst, src).then_inc(consts_loaded, 16)
            act.dma_start(bob, bo.rearrange("(o n) -> o n", o=1).to_broadcast([P, D])).then_inc(consts_loaded, 16)
            act.dma_start(gateS[0:EXPERTS, :], gate_w).then_inc(ffn_loaded, 16)
            act.dma_start(gateS[EXPERTS:EXPERTS + 1, :], s_gw).then_inc(ffn_loaded, 16)
            act.dma_start(wg, w_gu[:, :, 0:FF].rearrange("e d f -> d e f")).then_inc(ffn_loaded, 16)
            act.dma_start(wu, w_gu[:, :, FF:2 * FF].rearrange("e d f -> d e f")).then_inc(ffn_loaded, 16)
            act.dma_start(wd, w_down.rearrange("(c t) f n -> (t f) c n", t=2)).then_inc(ffn_loaded, 16)
            for t, s in enumerate((s_gate, s_up)):
                for b, (a, n) in enumerate(SBLK):
                    act.dma_start(shS[0:n, t, b, :], s[a:a + n, :]).then_inc(ffn_loaded, 16)
            act.dma_start(sdS, s_down).then_inc(ffn_loaded, 16)
            act.wait_ge(var_ready, 1)
            nc.scalar.activation(st[:, 3, :], st[:, 2, :], ACT.Sqrt).then_inc(std_ready, 1)
            for i, (_, dst, rows, cols) in enumerate(blocks):
                act.wait_ge(tr_full, i + 1)
                nc.scalar.activation(dst, T[i % 3][0:rows, 0:cols], ACT.Copy).then_inc(tr_taken, 1)
            for t, dst in enumerate((M, PV)):
                act.wait_ge(scaled_used, NCH * (t + 1))
                nc.scalar.activation(dst[:, 0:PIECE], R[0][:, :], ACT.Copy).then_inc(prod_taken, 1)
            act.wait_ge(gexp_ready, 1)
            nc.scalar.activation(comb[:, :, :], lg[:, :, :], ACT.Exp).then_inc(gexp_done, 1)
            for i in range(4):
                act.wait_ge(ct_full, i + 1)
                nc.scalar.activation(combT[:, i * 512:(i + 1) * 512], T[i % 2][0:EXPERTS + 1, :], ACT.Copy)\
                    .then_inc(ct_taken, 1)
            for k in range(4 * NJ):
                m = SBLK[k % NJ - NPAIR][1] if k % NJ >= NPAIR else P
                act.wait_ge(gu_full, k + 1)
                if k >= 2:
                    act.wait_ge(h_ready, 2 * (k - 1))
                nc.scalar.activation(sg[0:m, k % 2, :], R[k % 2][0:m, 0:512], ACT.Silu).then_inc(gate_read, 1)

            k_sign = 0
            act.wait_ge(down_taken, 4)

            def exponent(n):
                q = n // 4
                wd_ = width(q)
                act.wait_ge(max_ready, q + 1)
                if n >= 3:
                    act.wait_ge(tp_full, tcount(n - 3))
                nc.scalar.activation(E[:, n % 3, 0:wd_], S[:, n % 8, 0:wd_], ACT.Exp,
                                     bias=mbias[:, q % 2, n % 4:n % 4 + 1], scale=UP).then_inc(exp_done, 1)

            def take_transposed(n):
                q = n // 4
                base = tcount(n) - len(tpieces(q))
                if n >= 2:
                    act.wait_ge(z_done, n - 1)
                    act.wait_ge(mem_kept, n - 1)
                for i, (a, b) in enumerate(tpieces(q)):
                    act.wait_ge(tp_full, base + i + 1)
                    nc.scalar.activation(PT[:, n % 2, a * P:b * P], T[(base + i) % 3][:, 0:(b - a) * P], ACT.Copy)\
                        .then_inc(tp_taken, 1)

            def take_z(q):
                act.wait_ge(z_done, 4 * (q + 1))
                if q >= 1:
                    act.wait_ge(ring_full, RING["out", q - 1] + 1)
                nc.scalar.activation(zst[:], Z[:, :], ACT.Copy).then_inc(z_taken, 1)

            def signs(q, s):
                nonlocal k_sign
                wd_ = width(q)
                if s == 0:
                    act.wait_ge(first_ready, q - FIRST + 1)
                else:
                    act.wait_ge(step_ready, (ROUNDS - 1) * (q - FIRST) + s)
                for h in range(4):
                    if s == 0:
                        act.wait_ge(ring_taken, RING["score", 4 * q + h, len(pieces(q)) - 1] + 1)
                    if k_sign >= 2:
                        act.wait_ge(signs_summed, k_sign - 1)
                    nc.scalar.activation(junk[:, k_sign % 2, 0:wd_], S[:, 4 * (q % 2) + h, 0:wd_], ACT.Sign,
                                         bias=tg[:, q % 2, s, 0, h:h + 1], scale=NUDGE,
                                         accum_out=tg[:, q % 2, s, 1, h:h + 1]).then_inc(signs_summed, 1)
                    k_sign += 1

            for p in range(QUADS + 3):
                for h in range(4):
                    n = 4 * (p - 2) + h
                    if 0 <= n < 4 * QUADS:
                        exponent(n)
                    if h == 1 and 0 <= p - 3:
                        take_z(p - 3)
                    if 1 <= n <= 4 * QUADS:
                        take_transposed(n - 1)
                    if needs_search(p - 1):
                        signs(p - 1, h)

        @block.vector
        def _(dve):
            chain = [0]

            def link(ins):
                chain[0] += 1
                ins.then_inc(dve_chain, 1)
                dve.wait_ge(dve_chain, chain[0])

            V = nc.vector

            def bc(ap, n):
                return ap.rearrange("p (k o) -> p k o", o=1).to_broadcast([ap.shape[0], ap.shape[1], n])

            dve.wait_ge(x_loaded, 16)
            link(V.tensor_reduce(st[:, 0, :], acc[:, :, :], AXX, ALU.add))
            link(V.tensor_scalar(st[:, 0, :], st[:, 0, :], 1.0 / D, None, ALU.mult))
            link(V.tensor_tensor(XN[:, :, :], acc[:, :, :], bc(st[:, 0, :], D), ALU.subtract))
            link(V.tensor_tensor(xsq, XN[:, :, :], XN[:, :, :], ALU.mult))
            link(V.tensor_reduce(st[:, 1, :], xsq, AXX, ALU.add))
            V.tensor_scalar(st[:, 2, :], st[:, 1, :], 1.0 / D, EPS, ALU.mult, ALU.add).then_inc(var_ready, 1)
            dve.wait_ge(std_ready, 1)
            link(V.reciprocal(st[:, 4, :], st[:, 3, :]))
            link(V.tensor_tensor(st[:, 5, :], st[:, 4, :], st[:, 4, :], ALU.mult))
            link(V.tensor_tensor(st[:, 5, :], st[:, 5, :], st[:, 2, :], ALU.mult))
            link(V.tensor_scalar(st[:, 5, :], st[:, 5, :], -0.5, 1.5, ALU.mult, ALU.add))
            link(V.tensor_tensor(st[:, 4, :], st[:, 4, :], st[:, 5, :], ALU.mult))
            V.tensor_tensor(XN[:, :, :], XN[:, :, :], bc(st[:, 4, :], D), ALU.mult).then_inc(xn_ready, 1)
            dve.wait_ge(consts_loaded, 16 * 7)
            V.tensor_copy(identb[:], ident[:]).then_inc(casts_done, 1)
            V.tensor_copy(cmaskb[:], cmask[:]).then_inc(casts_done, 1)
            bo_rep = bob.rearrange("p (o d) -> p o d", o=1).to_broadcast([P, NB, D])
            link(V.tensor_tensor(acc[:, :, :], acc[:, :, :], bo_rep, ALU.add))

            dve.wait_ge(mixB_full, 1)
            link(V.tensor_scalar(preB.rearrange("p c k -> p (c k)"), R[0][:, 0:P], DH ** -0.5 * DOWN, None, ALU.mult))
            link(V.tensor_copy(postB.rearrange("p c k -> p (c k)"), R[0][:, P:2 * P]))
            for t in range(2):
                B = preB if t == 0 else postB
                for c in range(NCH):
                    k = NCH * t + c
                    if k >= 2:
                        dve.wait_ge(scaled_used, k - 1)
                    src = wT[:, 1, c, :] if t == 0 else woS[:, c, :]
                    if t == 0:
                        dve.wait_ge(tr_taken, n_att_tr)
                        V.tensor_tensor(scaledm[:, k % 2, :, :], bc(B[:, c, :], MEM),
                                        memT[:, 0, c, :].rearrange("p (o m) -> p o m", o=1).to_broadcast([P, HEADS, MEM]),
                                        ALU.mult).then_inc(scaled_ready, 1)
                    else:
                        dve.wait_ge(att_loaded, 16 * 22)
                    V.tensor_tensor(scaled[:, k % 2, :, :], bc(B[:, c, :], D),
                                    src.rearrange("p (o n) -> p o n", o=1).to_broadcast([P, HEADS, D]),
                                    ALU.mult).then_inc(scaled_ready, 1)
                dve.wait_ge(scaled_used, NCH * (t + 1))
                if t == 0:
                    link(V.tensor_copy(M[:, PIECE:], R[1][:, :]))
                    link(V.tensor_copy(Kmem[:], T[0][:, 0:HEADS * MEM]))
                else:
                    link(V.tensor_copy(PV[:, PIECE:], R[1][:, :]))
                    for i in range(3):
                        link(V.tensor_copy(MV[:, i * 512:(i + 1) * 512], T[i][0:MEM, :]))
                    link(V.tensor_copy(MV[:, 1536:2048], Z[0:MEM, :]))
                dve.sem_inc(prod_taken, 1)

            dve.wait_ge(gates_full, 1)
            link(V.tensor_copy(lg[:, :, :], T[0][:, 0:NB * 17].rearrange("p (b e) -> p b e", b=NB)))
            dve.sem_inc(gates_taken, 1)
            lo16, down = lg[:, :, 0:EXPERTS], rt[:, 3, :, :]
            index = rt[:, 2, :, :]
            m1, m2 = st[:, 0, :], st[:, 1, :]
            for e in range(EXPERTS):
                link(V.memset(index[:, :, e:e + 1], float(EXPERTS - e)))
            for t, m in ((0, m1), (1, m2)):
                left = lo16 if t == 0 else down
                link(V.tensor_reduce(m, left, AXX, ALU.max))
                link(V.tensor_tensor(rt[:, t, :, :], left, bc(m, EXPERTS), ALU.is_equal))
                link(V.tensor_tensor(rt[:, t, :, :], rt[:, t, :, :], index, ALU.mult))
                link(V.tensor_reduce(st[:, 2, :], rt[:, t, :, :], AXX, ALU.max))
                link(V.tensor_tensor(rt[:, t, :, :], index, bc(st[:, 2, :], EXPERTS), ALU.is_equal))
                if t == 0:
                    link(V.scalar_tensor_tensor(out=down, in0=rt[:, 0, :, :], scalar=LOWEST, in1=lo16,
                                                op0=ALU.mult, op1=ALU.add))
            link(V.tensor_tensor(rt[:, 0, :, :], rt[:, 0, :, :], rt[:, 1, :, :], ALU.add))
            link(V.tensor_tensor(lo16, lo16, bc(m1, EXPERTS), ALU.subtract))
            V.tensor_scalar(lg[:, :, 16:17], lg[:, :, 16:17], -1.0, None, ALU.mult).then_inc(gexp_ready, 1)
            dve.wait_ge(gexp_done, 1)
            ce = comb[:, :, 0:EXPERTS]
            link(V.tensor_tensor(ce, ce, rt[:, 0, :, :], ALU.mult))
            link(V.tensor_reduce(st[:, 2, :], ce, AXX, ALU.add))
            link(V.reciprocal(st[:, 3, :], st[:, 2, :]))
            link(V.tensor_tensor(ce, ce, bc(st[:, 3, :], EXPERTS), ALU.mult))
            link(V.tensor_scalar(comb[:, :, 16:17], comb[:, :, 16:17], 1.0, None, ALU.add))
            V.reciprocal(comb[:, :, 16:17], comb[:, :, 16:17]).then_inc(comb_ready, 1)

            for c in range(4):
                for j in range(NJ):
                    k = NJ * c + j
                    m = SBLK[j - NPAIR][1] if j >= NPAIR else P
                    dve.wait_ge(gate_read, k + 1)
                    if c >= 1:
                        dve.wait_ge(down_full, c)
                    V.tensor_tensor(su[0:m, k % 2, :], sg[0:m, k % 2, :], R[k % 2][0:m, 512:1024], ALU.mult)\
                        .then_inc(h_ready, 1)
                    dve.wait_ge(h_ready, 2 * k + 1)
                    V.tensor_tensor(H[0:m, j, :], su[0:m, k % 2, :], T[k % 2][0:m, :], ALU.mult).then_inc(h_ready, 1)
                dve.wait_ge(down_full, c + 1)
                V.tensor_tensor(acc[:, 4 * c:4 * c + 4, :], acc[:, 4 * c:4 * c + 4, :],
                                Z[:, :].rearrange("p (b d) -> p b d", b=4), ALU.add).then_inc(down_taken, 1)
            dve.wait_ge(down_taken, 4)
            for i in range(3):
                V.memset(T[i][:, :], 0.0).then_inc(t_banks_zeroed, 1)

            def general(n, target, link_):
                wd_ = width(n // 4)
                src = S[:, n % 8, 0:wd_]
                for i in range(TOPK // 8):
                    link_(V.max(t8[:], src))
                    if i < TOPK // 8 - 1:
                        link_(V.match_replace(out=Y[:, 0:wd_], in_to_replace=t8[:], in_values=src, imm_value=LOWEST))
                        src = Y[:, 0:wd_]
                link_(V.tensor_copy(target, t8[:, 7:8]))

            def take_scores(n):
                q = n // 4
                if q >= 2:
                    dve.wait_ge(probs_ready, n - 7)
                for i, (a, b) in enumerate(pieces(q)):
                    k = RING["score", n, i]
                    dve.wait_ge(ring_full, k + 1)
                    V.tensor_scalar(S[:, n % 8, a:b], R[k % 2][:, 0:b - a], 1.0, LOWEST, ALU.mult, ALU.max,
                                    accum_out=mxp[:, n % 8, i:i + 1]).then_inc(ring_taken, 1)

            def maxima(q):
                b = q % 2
                np_ = len(pieces(q))
                dve.wait_ge(ring_taken, RING["score", 4 * q + 3, np_ - 1] + 1)
                if q >= 2:
                    dve.wait_ge(exp_done, 4 * (q - 1))
                link(V.tensor_reduce(mxq[:, b, :], mxp[:, 4 * b:4 * b + 4, 0:np_], AXX, ALU.max))
                V.tensor_scalar(mbias[:, b, :], mxq[:, b, :], -UP, None, ALU.mult).then_inc(max_ready, 1)

            def take_queries(q):
                k = RING["query", q]
                dve.wait_ge(ring_full, k + 1)
                if needs_search(q - 2):
                    dve.wait_ge(squares_ready, q - 2 - FIRST + 1)
                V.tensor_copy(QT[:, q % 2, :], R[k % 2][:, 0:512]).then_inc(ring_taken, 1)

            def take_small(p):
                k = RING["small", p]
                dve.wait_ge(ring_full, k + 1)
                if needs_search(p):
                    if p >= FIRST + 2:
                        dve.wait_ge(first_ready, p - 2 - FIRST + 1)
                    ins = V.tensor_copy(sg2[:, p % 2, :], R[k % 2][:, 0:4])
                    if needs_search(p - 2):
                        ins.then_inc(squares_taken, 1)
                    else:
                        ins.then_inc(ring_taken, 1)
                if needs_search(p - 2):
                    if needs_search(p):
                        dve.wait_ge(squares_taken, p - FIRST - 1)
                    V.tensor_copy(failed[:], R[k % 2][0:1, 512:521]).then_inc(ring_taken, 1)
                    dve.wait_ge(ring_taken, k + 1)

            def below(n):
                q = n // 4
                wd_ = width(q)
                s = S[:, n % 8, 0:wd_]
                dve.wait_ge(marks_set, 2 * (q - FIRST + 1))
                V.scalar_tensor_tensor(out=Y[:, 0:wd_], in0=s, scalar=mark[:, q % 2, n % 4:n % 4 + 1], in1=s,
                                       op0=ALU.is_gt, op1=ALU.subtract, reverse1=True).then_inc(lowered, 1)

            def largest(n):
                q = n // 4
                dve.wait_ge(lowered, n - 4 * FIRST + 1)
                V.max(y17[:, q % 2, n % 4, 1:9], Y[:, 0:width(q)]).then_inc(largest_found, 1)

            def choose(n):
                q = n // 4
                dve.wait_ge(ranks_ready, q - FIRST + 1)
                dve.wait_ge(largest_found, n - 4 * FIRST + 1)
                V.scalar_tensor_tensor(out=pick[:, n % 2, 0:9], in0=y17[:, q % 2, n % 4, 0:9], scalar=1.0,
                                       in1=hot[:, q % 2, n % 4, 0:9], op0=ALU.mult, op1=ALU.mult,
                                       accum_out=thr[:, n % 8:n % 8 + 1]).then_inc(chosen, 1)

            def repair(n, any_failed):
                q, b, h = n // 4, (n // 4) % 2, n % 4
                wd_ = width(q)
                with dve.If(any_failed > 0):
                    beyond_9 = dve.value_load(failed[0:1, h:h + 1], min_val=0, max_val=2 * P)
                    with dve.If(beyond_9 > 0):
                        steps = [0]

                        def glink(ins):
                            steps[0] += 1
                            ins.then_inc(general_chain, 1)
                            dve.wait_ge(general_chain, steps[0])

                        dve.wait_ge(chosen, n - 4 * FIRST + 1)
                        glink(V.match_replace(out=Y[:, 0:wd_], in_to_replace=y17[:, b, h, 1:9],
                                              in_values=Y[:, 0:wd_], imm_value=LOWEST))
                        glink(V.max(y17[:, b, h, 9:17], Y[:, 0:wd_]))
                        glink(V.scalar_tensor_tensor(out=pick[:, n % 2, :], in0=y17[:, b, h, :], scalar=1.0,
                                                     in1=hot[:, b, h, :], op0=ALU.mult, op1=ALU.mult,
                                                     accum_out=thr[:, n % 8:n % 8 + 1]))
                        dve.sem_clear(general_chain)
                        beyond_17 = dve.value_load(failed[0:1, 4 + h:5 + h], min_val=0, max_val=2 * P)
                        with dve.If(beyond_17 > 0):
                            steps[0] = 0
                            general(n, thr[:, n % 8:n % 8 + 1], glink)
                            dve.sem_clear(general_chain)

            def weights(n):
                wd_ = width(n // 4)
                dve.wait_ge(exp_done, n + 1)
                if n >= 4 * FIRST:
                    dve.wait_ge(chosen, n - 4 * FIRST + 1)
                V.scalar_tensor_tensor(out=E[:, n % 3, 0:wd_], in0=S[:, n % 8, 0:wd_],
                                       scalar=thr[:, n % 8:n % 8 + 1], in1=E[:, n % 3, 0:wd_],
                                       op0=ALU.is_ge, op1=ALU.mult, accum_out=rsum[:, n % 8:n % 8 + 1])\
                    .then_inc(probs_ready, 1)

            def inverse(q):
                dve.wait_ge(probs_ready, 4 * (q + 1))
                V.reciprocal(rinv[:, q % 2, :], rsum[:, 4 * (q % 2):4 * (q % 2) + 4]).then_inc(inverted, 1)

            def add_out(q, h):
                k = RING["out", q]
                b = q // 4
                dve.wait_ge(ring_full, k + 1)
                if h == 0:
                    dve.wait_ge(inverted, q + 1)
                else:
                    dve.wait_ge(added, 3 * q + h)
                ins = V.scalar_tensor_tensor(out=acc[:, b, :], in0=R[k % 2][:, h * D:(h + 1) * D],
                                             scalar=rinv[:, q % 2, h:h + 1], in1=acc[:, b, :],
                                             op0=ALU.mult, op1=ALU.add)
                if h < 3:
                    ins.then_inc(added, 1)
                else:
                    ins.then_inc(ring_taken, 1)
                    dve.wait_ge(ring_taken, k + 1)
                    if q % 4 == 3:
                        dve.sem_inc(rows_ready, 1)

            take_queries(0)
            for p in range(QUADS + 3):
                q = p - 2
                search = needs_search(q)
                for h in range(4):
                    n = 4 * q + h
                    if search:
                        below(n)
                    if 0 <= n - 1 < 4 * QUADS:
                        weights(n - 1)
                    if search:
                        largest(n)
                    if 0 <= n + 7 < 4 * QUADS:
                        take_scores(n + 7)
                    if h == 0 and 0 <= p - 1 < QUADS:
                        maxima(p - 1)
                    if h == 0 and 0 <= q - 1 < QUADS:
                        inverse(q - 1)
                    if h == 2 and p + 1 < QUADS:
                        take_queries(p + 1)
                    if h == 0 and ("small", p) in RING:
                        take_small(p)
                        if search:
                            any_failed = dve.value_load(failed[0:1, 8:9], min_val=0, max_val=8 * P)
                    if search:
                        choose(n)
                        repair(n, any_failed)
                    elif 0 <= n < 4 * QUADS:
                        general(n, thr[:, n % 8:n % 8 + 1], link)
                    if h == 3 and 0 <= p - 3:
                        for i in range(4):
                            add_out(p - 3, i)

        @block.tensor
        def _(pe):
            mm, tr = nc.tensor.matmul, nc.tensor.transpose

            pe.wait_ge(consts_loaded, 16 * 7)
            for i, (parts, _, _, _) in enumerate(blocks):
                if i == 0:
                    pe.wait_ge(att_loaded, 16 * 22)
                if i == n_att_tr:
                    pe.wait_ge(ffn_loaded, 16 * 12)
                if i == n_w_tr:
                    pe.wait_ge(xn_ready, 1)
                if i >= 3:
                    pe.wait_ge(tr_taken, i - 2)
                at = 0
                for src, rows, cols in parts:
                    last = tr(T[i % 3][0:cols, at:at + rows], src, ident[0:rows, 0:rows])
                    at += rows
                last.then_inc(tr_full, 1)
            pe.wait_ge(tr_taken, n_att_tr)
            for t, m in enumerate((preS, postT)):
                for c in range(NCH):
                    last = mm(R[0][:, t * P + c * 16:t * P + (c + 1) * 16], sel[0:HEADS, c, :], m, start=True, stop=True)
            last.then_inc(mixB_full, 1)
            pe.wait_ge(tr_taken, n_tr)
            ready = 0
            for t in range(2):
                if t == 1:
                    pe.wait_ge(prod_taken, 2)
                for c in range(NCH):
                    k = NCH * t + c
                    ready += 2 if t == 0 else 1
                    pe.wait_ge(scaled_ready, ready)
                    lhs = wT[:, 0, c, :] if t == 0 else wT[:, 2, c, :]
                    for i in range(4):
                        last = mm(R[i // 2][:, (i % 2) * 512:(i % 2 + 1) * 512], lhs,
                                  scaled[:, k % 2, 4 * i:4 * i + 4, :].rearrange("p k n -> p (k n)"),
                                  start=(c == 0), stop=(c == NCH - 1))
                    if t == 0:
                        last = mm(T[0][:, 0:HEADS * MEM], lhs, scaledm[:, k % 2, :, :].rearrange("p k m -> p (k m)"),
                                  start=(c == 0), stop=(c == NCH - 1))
                    else:
                        for i in range(4):
                            bank = T[i] if i < 3 else Z
                            last = mm(bank[0:MEM, :], memT[:, 1, c, :],
                                      scaled[:, k % 2, 4 * i:4 * i + 4, :].rearrange("p k n -> p (k n)"),
                                      start=(c == 0), stop=(c == NCH - 1))
                    last.then_inc(scaled_used, 1)
            pe.wait_ge(prod_taken, 4)
            for b in range(NB):
                last = mm(T[0][:, 17 * b:17 * (b + 1)], xnT[:, b * P:(b + 1) * P], gateT, start=True, stop=True)
            last.then_inc(gates_full, 1)
            pe.wait_ge(comb_ready, 1)
            pe.wait_ge(gates_taken, 1)
            for i in range(4):
                if i >= 2:
                    pe.wait_ge(ct_taken, i - 1)
                for b in range(4):
                    last = tr(T[i % 2][0:17, b * P:(b + 1) * P], comb[:, 4 * i + b, :], ident[:, :])
                last.then_inc(ct_full, 1)
            pe.wait_ge(ct_taken, 4)
            for c in range(4):
                cols = xnT[:, c * 512:(c + 1) * 512]
                for j in range(NJ):
                    k = NJ * c + j
                    if j < NPAIR:
                        m = P
                        lg_, lu_ = (a[:, 2 * j:2 * j + 2, :].rearrange("p e f -> p (e f)") for a in (wg, wu))
                        ls_ = sel[0:17, j, :]
                    else:
                        a0, m = SBLK[j - NPAIR]
                        lg_, lu_ = (shT[:, t, j - NPAIR, 0:m] for t in range(2))
                        ls_ = sel[0:17, NPAIR, 0:m]
                    if k >= 2:
                        pe.wait_ge(h_ready, 2 * (k - 1))
                    mm(R[k % 2][0:m, 0:512], lg_, cols, start=True, stop=True)
                    mm(R[k % 2][0:m, 512:1024], lu_, cols, start=True, stop=True)
                    mm(T[k % 2][0:m, :], ls_, combT[:, c * 512:(c + 1) * 512], start=True, stop=True)\
                        .then_inc(gu_full, 1)
                pe.wait_ge(h_ready, 2 * NJ * (c + 1))
                if c >= 1:
                    pe.wait_ge(down_taken, c)
                for b in range(4):
                    for j in range(NJ):
                        m = SBLK[j - NPAIR][1] if j >= NPAIR else P
                        rhs = wd[:, j, :] if j < NPAIR else sdT[0:m, j - NPAIR, :]
                        last = mm(Z[:, b * D:(b + 1) * D], H[0:m, j, b * P:(b + 1) * P], rhs,
                                  start=(j == 0), stop=(j == NJ - 1))
                last.then_inc(down_full, 1)

            pe.wait_ge(down_taken, 4)
            pe.wait_ge(t_banks_zeroed, 3)
            pe.wait_ge(casts_done, 2)
            pe.wait_ge(ones_set, 1)

            def slot(item):
                k = RING[item]
                if k >= 2:
                    pe.wait_ge(ring_taken, k - 1)
                return R[k % 2]

            def queries(q):
                r, ps = q // 4, slot(("query", q))
                for h in range(4):
                    k = 4 * (q % 4) + h
                    last = mm(ps[:, h * P:(h + 1) * P], M[:, k * D:(k + 1) * D], xnT[:, r * P:(r + 1) * P],
                              start=True, stop=True)
                last.then_inc(ring_full, 1)

            def small(p):
                ps = slot(("small", p))
                if needs_search(p):
                    pe.wait_ge(squares_ready, p - FIRST + 1)
                    for h in range(4):
                        last = mm(ps[:, h:h + 1], sq[:, h * P:(h + 1) * P], ones[:, 0:1], start=True, stop=True)
                if needs_search(p - 2):
                    pe.wait_ge(fails_ready, p - 2 - FIRST + 1)
                    mm(ps[0:1, 512:520], ones[:, 0:1], fail[:, :], start=True, stop=True)
                    for h in range(4):
                        last = mm(ps[0:1, 520:521], ones[:, 0:1], fail[:, h:h + 1], start=(h == 0), stop=(h == 3))
                last.then_inc(ring_full, 1)

            def scores(n):
                q, r, h = n // 4, n // 16, n % 4
                keys = P * (r + 1)
                if h == 0:
                    pe.wait_ge(ring_taken, RING["query", q] + 1)
                for i, (a, b) in enumerate(pieces(q)):
                    ps = slot(("score", n, i))
                    for s in range(a, b, 512):
                        e = min(s + 512, b)
                        ek = min(e, keys)
                        if ek > s:
                            diag = s <= r * P < ek
                            last = mm(ps[:, s - a:ek - a], QT[:, q % 2, h * P:(h + 1) * P], xnT[:, s:ek],
                                      start=True, stop=not diag)
                            if diag:
                                last = mm(ps[:, r * P - a:keys - a], identb[:], cmaskb[:], start=False, stop=True)
                        if e > keys:
                            k = n % 16
                            last = mm(ps[:, keys - a:e - a], xnT[:, r * P:(r + 1) * P], Kmem[:, k * MEM:(k + 1) * MEM],
                                      start=True, stop=True)
                    last.then_inc(ring_full, 1)

            def transposes(n, first, end):
                q = n // 4
                nk = q // 4 + 1
                base = tcount(n) - len(tpieces(q))
                if first == 0:
                    pe.wait_ge(probs_ready, n + 1)
                for i, (a, b) in list(enumerate(tpieces(q)))[first:end]:
                    if base + i >= 3:
                        pe.wait_ge(tp_taken, base + i - 2)
                    for j in range(a, b):
                        cols = P if j < nk else MEM
                        last = tr(T[(base + i) % 3][0:cols, (j - a) * P:(j - a + 1) * P],
                                  E[:, n % 3, j * P:j * P + cols], ident[:])
                    last.then_inc(tp_full, 1)

            def values(n):
                q, h = n // 4, n % 4
                nk = q // 4 + 1
                if h == 0 and q >= 1:
                    pe.wait_ge(z_taken, q)
                pe.wait_ge(tp_taken, tcount(n))
                for j in range(nk):
                    last = mm(Z[:, h * P:(h + 1) * P], XN[:, j, :], PT[:, n % 2, j * P:(j + 1) * P],
                              start=(j == 0), stop=(j == nk - 1))
                last.then_inc(z_done, 1)

            def project(q):
                ps = slot(("out", q))
                pe.wait_ge(z_taken, q + 1)
                pe.wait_ge(mem_kept, 4 * (q + 1))
                for h in range(4):
                    k = 4 * (q % 4) + h
                    mm(ps[:, h * D:(h + 1) * D], zst[:, h * P:(h + 1) * P], PV[:, k * D:(k + 1) * D],
                       start=True, stop=False)
                    last = mm(ps[:, h * D:(h + 1) * D], memPT[:, q % 2, h, :], MV[:, k * D:(k + 1) * D],
                              start=False, stop=True)
                last.then_inc(ring_full, 1)

            queries(0)
            for p in range(QUADS + 3):
                for h in range(4):
                    n = 4 * (p - 2) + h
                    turn = 1 <= n <= 4 * QUADS
                    if turn:
                        transposes(n - 1, 0, 3 if h else 5)
                    if h == 0 and ("small", p) in RING:
                        small(p)
                    if h == 2 and p + 1 < QUADS:
                        queries(p + 1)
                    if h == 3 and 0 <= p - 3:
                        project(p - 3)
                    if p < QUADS:
                        scores(4 * p + h)
                    if turn:
                        if h:
                            transposes(n - 1, 3, 5)
                        values(n - 1)


_INS = ["L0_attn_x", "L0_attn_Wq", "L0_attn_Wk", "L0_attn_Wv", "L0_attn_pre_proj", "L0_attn_post_proj",
        "L0_attn_mem_k", "L0_attn_mem_v", "L0_attn_Wo", "L0_attn_bo", "L0_ffn_gate_w", "L0_ffn_w_gate_up",
        "L0_ffn_w_down", "L0_ffn_shared_w_gate", "L0_ffn_shared_w_up", "L0_ffn_shared_w_down",
        "L0_ffn_shared_gate_w"]


def shape_tables():
    import numpy as np

    def over(z):
        return 0.5 * math.erfc(z / math.sqrt(2.0))

    def density(z):
        return math.exp(-z * z / 2) / math.sqrt(2 * math.pi)

    sel = np.zeros((EXPERTS + 1, 9, P), np.float32)
    for c in range(8):
        for p in range(P):
            sel[2 * c + p // DH, c, p] = 1.0
    sel[EXPERTS, 8, :] = 1.0
    i = np.arange(P)
    cmask = np.where(i[None, :] > i[:, None], np.float32(MASKED), np.float32(0.0)).astype(np.float32)
    spread = 4.6
    z = np.zeros(N)
    kap = np.ones(N)
    for r in range(P, N):
        lo, hi = -2.0, 5.0
        for _ in range(40):
            mid = (lo + hi) / 2
            above = (r + 1) * over(mid) + MEM * over(mid / spread)
            lo, hi = (mid, hi) if above > AIM else (lo, mid)
        z[r] = mid
        kap[r] = 0.5 / ((r + 1) * density(mid) + MEM * density(mid / spread) / spread)
    return {"ident": np.eye(P, dtype=np.float32), "sel": sel.reshape(EXPERTS + 1, 9 * P), "cmask": cmask,
            "nz": np.ascontiguousarray(-z.reshape(NB, P).T).astype(np.float32),
            "kap": np.ascontiguousarray(kap.reshape(NB, P).T).astype(np.float32),
            "iota": np.tile(np.arange(17, dtype=np.float32), (P, 4))}


def kernel(**inputs):
    import numpy as np
    import concourse.bacc as bacc
    from concourse.bass_utils import run_bass_kernel_spmd

    nc = bacc.Bacc("TRN2", target_bir_lowering=False, num_devices=1)
    arrays = {f"in_{n}": np.ascontiguousarray(inputs[n]) for n in _INS}
    arrays["in_L0_attn_x"] = arrays["in_L0_attn_x"].reshape(N, D)
    arrays.update({f"tab_{k}": v for k, v in shape_tables().items()})
    args = [nc.dram_tensor(k, v.shape, mybir.dt.from_np(v.dtype), kind="ExternalInput").ap()
            for k, v in arrays.items()]
    out = nc.dram_tensor("out_y", (N, D), F32, kind="ExternalOutput").ap()
    build(nc, *args, out)
    r = run_bass_kernel_spmd(nc, [arrays], core_ids=[0])
    return r.results[0]["out_y"].reshape(1, N, D)
```

```python
import math
from contextlib import ExitStack

import concourse.bass as bass
from concourse import mybir

F32 = mybir.dt.float32
BF16 = mybir.dt.bfloat16
I32 = mybir.dt.int32
ALU = mybir.AluOpType
ACT = mybir.ActivationFunctionType
AXX = mybir.AxisListType.X

N = 2048
D = 128
P = 128
NB = N // P
HEADS = 16
DH = 64
MEM = 16
TOPK = 64
NCH = HEADS * DH // P
INNER = HEADS * DH
EXPERTS = 16
FF = 64
SHARED = 352
NPAIR = EXPERTS // 2
SBLK = [(0, 128), (128, 128), (256, 96)]
NJ = NPAIR + len(SBLK)
EPS = 1e-5
SCALE_BITS = 40
DOWN = 2.0 ** -SCALE_BITS
UP = 2.0 ** SCALE_BITS
MASKED = -2.0
LOWEST = -3.0e38
QUADS = NB * 4
WMAX = N + MEM
PIECE = 1024
NBLK = NB + 1
FIRST = 4
ACT_KEEPS = 4 * QUADS * 3 // 8
AIM = 60.2
NEAR = 4.1
ROUNDS = 4
NUDGE = 1.0 - 2.0 ** -24
NEXT = 1.0 + 0.75 * 2.0 ** -23


PARTS = 3 * (EXPERTS + 1)


def width(q):
    return P * (q // 4 + 1) + MEM


def pieces(q):
    w = width(q)
    return [(a, min(a + PIECE, w)) for a in range(0, w, PIECE)]


def tpieces(q):
    nb = q // 4 + 2
    return [(a, min(a + 4, nb)) for a in range(0, nb, 4)]


def ring_items():
    items = [("query", 0)]
    for p in range(QUADS + 3):
        for h in range(4):
            if h == 2 and p + 1 < QUADS:
                items.append(("query", p + 1))
            if h == 3 and 0 <= p - 3 < QUADS:
                items.append(("out", p - 3))
            n = 4 * p - 1 + h
            if 0 <= n < 4 * QUADS:
                items += [("score", n, i) for i in range(len(pieces(n // 4)))]
    return items


def needs_search(q):
    return FIRST <= q < QUADS


def small_items():
    items = []
    for p in range(QUADS + 3):
        if needs_search(p - 2):
            items.append(("failures", 2 * (p - 2)))
        if needs_search(p):
            items.append(("squares", p))
        if needs_search(p - 2):
            items.append(("failures", 2 * (p - 2) + 1))
    return items


def search_order():
    order = []
    for m in range(-8, 4 * QUADS):
        for u, s in ((m // 2 + 1, 2 + m % 2), (m // 2 + 2, m % 2)):
            if needs_search(u // 2):
                order.append((u, s, m))
    return order


RING = {item: i for i, item in enumerate(ring_items())}
SMALL = {item: i for i, item in enumerate(small_items())}
TURN = {(u, s): i for i, (u, s, _) in enumerate(search_order())}
STEP = {(u, s): i for i, (u, s) in enumerate((u, s) for u, s, _ in search_order() if s < ROUNDS - 1)}


def rounds_in(m):
    return [(u, s) for u, s, slot in search_order() if slot == m]


def tcount(n):
    return sum(4 * len(tpieces(q)) for q in range(n // 4)) + (n % 4 + 1) * len(tpieces(n // 4))


def build(nc, x, wq, wk, wv, pre, post, mem_k, mem_v, wo, bo, gate_w, w_gu, w_down, s_gate, s_up, s_down,
          s_gw, ident_d, sel_d, cmask_d, nz_d, kap_d, iota_d, out):
    ctx = ExitStack()
    with ctx:
        def sb(name, shape, dt=F32):
            return ctx.enter_context(nc.sbuf_tensor(name, shape, dt))

        def sem(name):
            return ctx.enter_context(nc.semaphore(name))

        S = sb("S", [P, 8, WMAX])
        E = sb("E", [P, 3, WMAX])
        Y = sb("Y", [P, WMAX])
        junk = sb("junk", [P, 2, WMAX], BF16)
        PT = sb("PT", [P, 2, NBLK * P])
        xnT = sb("xnT", [P, N])
        XN = sb("XN", [P, NB, D])
        M = sb("M", [P, HEADS * D])
        PV = sb("PV", [P, HEADS * D])
        MV = sb("MV", [MEM, HEADS * D])
        Kmem = sb("Kmem", [P, HEADS * MEM])
        acc = sb("acc", [P, NB, D])
        QT = sb("QT", [P, 2, 4 * P])
        sq = sb("sq", [P, 4 * P])
        zst = sb("zst", [P, 4 * P])
        ident = sb("ident", [P, P])
        identb = sb("identb", [P, P], BF16)
        cmask = sb("cmask", [P, P])
        cmaskb = sb("cmaskb", [P, P], BF16)
        ones = sb("ones", [P, 1])
        iota = sb("iota", [P, 4, 17])
        powers = sb("powers", [P, 2, 4])

        nz = sb("nz", [P, NB])
        kap = sb("kap", [P, NB])
        mxp = sb("mxp", [P, 8, 3])
        mxq = sb("mxq", [P, 2, 4])
        mbias = sb("mbias", [P, 2, 4])
        sg2 = sb("sg2", [P, 2, 4])
        tg = sb("tg", [P, 2, ROUNDS, 2, 4])
        diff = sb("diff", [P, 2, 2, 4])
        slope = sb("slope", [P, 2, 4])
        prior = sb("prior", [P, 2, 2, 4])
        far = sb("far", [P, 2, 4])
        inverse_ = sb("inverse_", [P, 4])
        sigma = sb("sigma", [P, 4])
        miss = sb("miss", [P, 3, 4])
        move = sb("move", [P, 4])
        raw = sb("raw", [P, 3, 4])
        mark = sb("mark", [P, 2, 4])
        beyond = sb("beyond", [P, 2, 2])
        shift = sb("shift", [P, 2, 2])
        tiny = sb("tiny", [P, 2, 2])
        rank = sb("rank", [P, 4])
        off = sb("off", [P, 2, 2])
        hot = sb("hot", [P, 2, 4, 17])
        fail = sb("fail", [P, 2, 4])
        failed = sb("failed", [1, 5], I32)
        y17 = sb("y17", [P, 2, 4, 17])
        t8 = sb("t8", [P, 8])
        pick = sb("pick", [P, 2, 17])
        thr = sb("thr", [P, 8])
        rsum = sb("rsum", [P, 8])
        rinv = sb("rinv", [P, 2, 4])
        memPT = sb("memPT", [MEM, 2, 4, P])
        st = sb("st", [P, 8, NB])

        Sf = S[:, :, :].rearrange("p a b -> p (a b)")
        Ef = E[:, :, :].rearrange("p a b -> p (a b)")
        PTf = PT[:, :, :].rearrange("p a b -> p (a b)")
        wqkv = Sf[:, 0:3 * INNER].rearrange("p (t n) -> p t n", t=3)
        wT = Sf[:, 3072:3072 + 3 * INNER].rearrange("p (t c n) -> p t c n", t=3, c=NCH)
        woS = Sf[:, 6144:7168].rearrange("p (c n) -> p c n", c=NCH)
        memS = Sf[:, 7168:7424].rearrange("p (t n) -> p t n", t=2)
        memT = Sf[:, 7424:7680].rearrange("p (t c m) -> p t c m", t=2, c=NCH)
        preB = Sf[:, 7680:7808].rearrange("p (c k) -> p c k", c=NCH)
        postB = Sf[:, 7808:7936].rearrange("p (c k) -> p c k", c=NCH)
        preS = Sf[0:HEADS, 7936:7952]
        postS = Sf[0:HEADS, 7952:7968]
        postT = Sf[0:HEADS, 7968:7984]
        gateS = Sf[0:EXPERTS + 1, 7984:8112]
        gateT = Sf[:, 8112:8129]
        sel = Sf[0:PARTS, 8192:8192 + 9 * P].rearrange("p (c n) -> p c n", c=9)
        wg = Sf[:, 9344:10368].rearrange("p (e f) -> p e f", e=EXPERTS)
        wu = Sf[:, 10368:11392].rearrange("p (e f) -> p e f", e=EXPERTS)
        wd = Sf[:, 11392:12416].rearrange("p (c n) -> p c n", c=NPAIR)
        shS = Sf[:, 12416:12416 + 6 * P].rearrange("p (t b n) -> p t b n", t=2, b=3)
        shT = Sf[:, 13184:13184 + 6 * P].rearrange("p (t b n) -> p t b n", t=2, b=3)
        sdS = Sf[:, 13952:13952 + SHARED]
        sdT = Sf[:, 14304:14304 + 3 * P].rearrange("p (b n) -> p b n", b=3)
        lg = Sf[:, 14688:14688 + NB * 17].rearrange("p (b e) -> p b e", b=NB)
        comb = Sf[:, 14960:14960 + NB * 17].rearrange("p (b e) -> p b e", b=NB)
        rt = Sf[:, 15232:15232 + 4 * NB * EXPERTS].rearrange("p (t b e) -> p t b e", t=4, b=NB)
        scaled = Ef[:, 0:4096].rearrange("p (t k n) -> p t k n", t=2, k=HEADS)
        scaledm = Ef[:, 4096:4608].rearrange("p (t k m) -> p t k m", t=2, k=HEADS)
        mvT = Ef[:, 4736:4992]
        bob = Ef[:, 4608:4736]
        H = Ef[:, 0:5632].rearrange("p (j n) -> p j n", j=NJ)
        sg = PTf[:, 0:1024].rearrange("p (t n) -> p t n", t=2)
        su = PTf[:, 1024:2048].rearrange("p (t n) -> p t n", t=2)
        parts3 = PTf[:, 2176:2176 + NB * PARTS].rearrange("p (b e) -> p b e", b=NB)
        partb = junk[:, 0, 0:NB * 17].rearrange("p (b e) -> p b e", b=NB)
        selb = junk[0:PARTS, 0, 512:512 + 9 * P].rearrange("p (c n) -> p c n", c=9)
        combT = junk[0:PARTS, 1, 0:N]
        xsq = PTf[:, 2048:4096].rearrange("p (b d) -> p b d", b=NB)

        R = [ctx.enter_context(nc.psum_tensor(f"R{i}", [P, PIECE], F32)) for i in range(2)]
        T = [ctx.enter_context(nc.psum_tensor(f"T{i}", [P, 512], F32)) for i in range(3)]
        F = T[2]
        Z = ctx.enter_context(nc.psum_tensor("Z", [P, 512], F32))

        x_loaded, consts_loaded, att_loaded, ffn_loaded = (sem(s) for s in (
            "x_loaded", "consts_loaded", "att_loaded", "ffn_loaded"))
        ones_set = sem("ones_set")
        casts_done = sem("casts_done")
        var_ready = sem("var_ready")
        std_ready = sem("std_ready")
        xn_ready = sem("xn_ready")
        tr_full, tr_taken = sem("tr_full"), sem("tr_taken")
        mixB_full = sem("mixB_full")
        scaled_ready, scaled_used = sem("scaled_ready"), sem("scaled_used")
        prod_taken = sem("prod_taken")
        mvT_ready, mv_full = sem("mvT_ready"), sem("mv_full")
        gates_full, comb_ready = sem("gates_full"), sem("comb_ready")
        gates_taken = sem("gates_taken")
        gexp_ready, gexp_done = sem("gexp_ready"), sem("gexp_done")
        ct_full, ct_taken = sem("ct_full"), sem("ct_taken")
        gu_full, gate_read, h_ready = sem("gu_full"), sem("gate_read"), sem("h_ready")
        down_full, down_taken = sem("down_full"), sem("down_taken")
        dve_chain, pool_chain = sem("dve_chain"), sem("pool_chain")
        t_banks_zeroed = sem("t_banks_zeroed")

        ring_full, ring_taken = sem("ring_full"), sem("ring_taken")
        tp_full, tp_taken = sem("tp_full"), sem("tp_taken")
        z_done, z_taken = sem("z_done"), sem("z_taken")
        exp_done = sem("exp_done")
        signs_summed = sem("signs_summed")
        mark_steps, marks_set = sem("mark_steps"), sem("marks_set")
        squares_ready = sem("squares_ready")
        first_ready, step_ready = sem("first_ready"), sem("step_ready")
        small_full, small_taken = sem("small_full"), sem("small_taken")
        lowered, largest_found, chosen = sem("lowered"), sem("largest_found"), sem("chosen")
        inverted, added = sem("inverted"), sem("added")
        rank_steps = sem("rank_steps")
        ranks_ready, fails_ready = sem("ranks_ready"), sem("fails_ready")
        max_ready = sem("max_ready")
        probs_ready = sem("probs_ready")
        rows_ready = sem("rows_ready")
        general_chain = sem("general_chain")
        stored = sem("stored")
        mem_kept = sem("mem_kept")

        blocks = []
        for t in range(3):
            for c0 in range(0, NCH, 4):
                blocks.append(([(wqkv[:, t, (c0 + i) * P:(c0 + i + 1) * P], P, P) for i in range(4)],
                               wT[:, t, c0:c0 + 4, :].rearrange("p c n -> p (c n)"), P, 512))
        blocks.append(([(memS[:, t, :], P, P) for t in range(2)],
                       memT[:, :, :, :].rearrange("p t c m -> p (t c m)"), P, 256))
        blocks.append(([(postS, HEADS, HEADS)], postT, HEADS, HEADS))
        n_att_tr = len(blocks)
        blocks.append(([(gateS, EXPERTS + 1, P)], gateT, P, EXPERTS + 1))
        for t in range(2):
            blocks.append(([(shS[0:n, t, b, :], n, P) for b, (_, n) in enumerate(SBLK)],
                           shT[:, t, :, :].rearrange("p b n -> p (b n)")[:, 0:SHARED], P, SHARED))
        for b, (a, n) in enumerate(SBLK):
            blocks.append(([(sdS[:, a:a + n], P, n)], sdT[0:n, b, :], n, P))
        n_w_tr = len(blocks)
        for b in range(0, NB, 4):
            blocks.append(([(XN[:, b + i, :], P, P) for i in range(4)], xnT[:, b * P:(b + 4) * P], P, 512))
        n_tr = len(blocks)

        block = ctx.enter_context(nc.Block())

        @block.sync
        def _(sp):
            sp.dma_start(acc[:, :, :], x.rearrange("(b p) d -> p b d", p=P)).then_inc(x_loaded, 16)
            for t, w in enumerate((wq, wk, wv)):
                sp.dma_start(wqkv[:, t, :], w).then_inc(att_loaded, 16)
            sp.dma_start(woS, wo.rearrange("(c p) n -> p c n", p=P)).then_inc(att_loaded, 16)
            sp.dma_start(preS, pre).then_inc(att_loaded, 16)
            sp.dma_start(postS, post).then_inc(att_loaded, 16)
            for t, m in enumerate((mem_k, mem_v)):
                for c in range(NCH):
                    sp.dma_start(memS[c * MEM:(c + 1) * MEM, t, :].rearrange("m (t e) -> m t e", t=2),
                                 m[2 * c:2 * c + 2].rearrange("t m e -> m t e")).then_inc(att_loaded, 16)
            for b in range(NB):
                sp.wait_ge(rows_ready, b + 1)
                sp.dma_start(out[b * P:(b + 1) * P, :], acc[:, b, :]).then_inc(stored, 16)
            sp.wait_ge(stored, 16 * NB)

        @block.gpsimd
        def _(pool):
            chain = [0]

            def link(ins):
                chain[0] += 1
                ins.then_inc(pool_chain, 1)
                pool.wait_ge(pool_chain, chain[0])

            def beside(ins):
                chain[0] += 1
                ins.then_inc(pool_chain, 1)

            nc.gpsimd.memset(ones[:], 1.0).then_inc(ones_set, 1)
            nc.gpsimd.memset(powers[:, 0, :], 0.5).then_inc(ones_set, 1)
            nc.gpsimd.memset(powers[:, 1, :], -1.0).then_inc(ones_set, 1)
            nc.gpsimd.memset(prior[:, 0, 1, :], 1.0).then_inc(ones_set, 1)
            nc.gpsimd.memset(prior[:, 1, 1, :], 1.0).then_inc(ones_set, 1)
            pool.wait_ge(ones_set, 5)

            def start(q):
                pool.wait_ge(ring_taken, RING["query", q] + 1)
                if q > FIRST:
                    pool.wait_ge(small_full, SMALL["squares", q - 1] + 1)
                nc.gpsimd.tensor_tensor(sq[:], QT[:, q % 2, :], QT[:, q % 2, :], ALU.mult).then_inc(squares_ready, 1)

            G = nc.gpsimd

            def first_threshold(q):
                b, r = q % 2, q // 4
                pool.wait_ge(small_taken, SMALL["squares", q] + 1)
                link(G.tensor_tensor(sigma[:], sg2[:, b, :], powers[:, 0, :], ALU.pow))
                link(G.tensor_scalar(prior[:, b, 0, :], sigma[:], kap[:, r:r + 1], None, ALU.mult))
                G.tensor_scalar(tg[:, b, 0, 0, :], sigma[:], nz[:, r:r + 1], None, ALU.mult).then_inc(first_ready, 1)
                pool.wait_ge(first_ready, q - FIRST + 1)

            def step(u, s):
                q, c = u // 2, 2 * (u % 2)
                b, c = q % 2, slice(c, c + 2)
                pool.wait_ge(signs_summed, 2 * (TURN[u, s] + 1))
                first = 1 if s < 2 else 0
                d, same = diff[:, max(s - 1, 0), :, c], far[:, 0:1, c].to_broadcast([P, 2, 2])
                if s > 0:
                    beside(G.tensor_tensor(d, tg[:, b, s, :, c], tg[:, b, s - 1, :, c], ALU.subtract))
                link(G.tensor_scalar(miss[:, s, c], tg[:, b, s, 1, c], float(2 * AIM - width(q)), None, ALU.subtract))
                both = miss[:, s:s + 1, c].to_broadcast([P, 2 - first, 2])
                link(G.tensor_tensor(far[:, first:2, c], miss[:, s - 1 + first:s + 1, c], both, ALU.mult))
                link(G.tensor_scalar(far[:, first:2, c], far[:, first:2, c], (2 * NEAR) ** 2, None, ALU.is_gt))
                if s == 2:
                    link(G.tensor_tensor(diff[:, 0, :, c], diff[:, 0, :, c], same, ALU.mult))
                    link(G.tensor_tensor(d, d, diff[:, 0, :, c], ALU.add))
                beside(G.tensor_tensor(move[:, c], far[:, 1, c], miss[:, s, c], ALU.mult))
                m = prior[:, b, 0, c]
                if s > 0:
                    dg = diff[:, s - 1, 1:2, c].to_broadcast([P, 2, 2])
                    link(G.tensor_tensor(slope[:, :, c], d, dg, ALU.mult))
                    link(G.tensor_tensor(slope[:, :, c], slope[:, :, c], prior[:, b, :, c], ALU.add))
                    beside(G.tensor_tensor(move[:, c], move[:, c], slope[:, 0, c], ALU.mult))
                    link(G.tensor_tensor(inverse_[:, c], slope[:, 1, c], powers[:, 1, c], ALU.pow))
                    m = inverse_[:, c]
                else:
                    pool.wait_ge(pool_chain, chain[0])
                link(G.tensor_tensor(move[:, c], move[:, c], m, ALU.mult))
                if s < ROUNDS - 2:
                    ins = G.tensor_tensor(tg[:, b, s + 1, 0, c], tg[:, b, s, 0, c], move[:, c], ALU.subtract)
                else:
                    link(G.tensor_tensor(raw[:, 0, c], tg[:, b, s, 0, c], move[:, c], ALU.subtract))
                    link(G.tensor_scalar(raw[:, 1, c], raw[:, 0, c], 3.0, None, ALU.mult))
                    link(G.tensor_tensor(raw[:, 2, c], raw[:, 1, c], raw[:, 0, c], ALU.subtract))
                    ins = G.tensor_tensor(tg[:, b, s + 1, 0, c], raw[:, 1, c], raw[:, 2, c], ALU.subtract)
                ins.then_inc(step_ready, 1)
                pool.wait_ge(step_ready, STEP[u, s] + 1)

            def keep_memory(n):
                q, nk = n // 4, n // 16 + 1
                pool.wait_ge(tp_taken, tcount(n))
                pool.wait_ge(mem_kept, n)
                if q >= 2:
                    pool.wait_ge(ring_full, RING["out", q - 2] + 1)
                nc.gpsimd.tensor_copy(memPT[:, q % 2, n % 4, :], PT[0:MEM, n % 2, nk * P:(nk + 1) * P])\
                    .then_inc(mem_kept, 1)

            pool.wait_ge(consts_loaded, 16 * 9)
            for p in range(QUADS + 3):
                for h in range(4):
                    m = 4 * (p - 2) + h
                    if ACT_KEEPS <= m - 2 < 4 * QUADS:
                        keep_memory(m - 2)
                    for u, s in rounds_in(m):
                        if s < ROUNDS - 1:
                            step(u, s)
                    if h == 2 and needs_search(p):
                        first_threshold(p)
                if needs_search(p + 1):
                    start(p + 1)

        @block.scalar
        def _(act):
            sel_src = sel_d.rearrange("k (c n) -> k c n", c=9)
            for i in range(3):
                act.dma_start(sel[17 * i:17 * (i + 1)], sel_src).then_inc(consts_loaded, 16)
            for dst, src in ((ident[:], ident_d),
                             (cmask[:], cmask_d), (nz[:], nz_d), (kap[:], kap_d),
                             (iota[:, :, :], iota_d.rearrange("p (h k) -> p h k", h=4))):
                act.dma_start(dst, src).then_inc(consts_loaded, 16)
            act.dma_start(bob, bo.rearrange("(o n) -> o n", o=1).to_broadcast([P, D])).then_inc(consts_loaded, 16)
            act.dma_start(gateS[0:EXPERTS, :], gate_w).then_inc(ffn_loaded, 16)
            act.dma_start(gateS[EXPERTS:EXPERTS + 1, :], s_gw).then_inc(ffn_loaded, 16)
            act.dma_start(wg, w_gu[:, :, 0:FF].rearrange("e d f -> d e f")).then_inc(ffn_loaded, 16)
            act.dma_start(wu, w_gu[:, :, FF:2 * FF].rearrange("e d f -> d e f")).then_inc(ffn_loaded, 16)
            act.dma_start(wd, w_down.rearrange("(c t) f n -> (t f) c n", t=2)).then_inc(ffn_loaded, 16)
            for t, s in enumerate((s_gate, s_up)):
                for b, (a, n) in enumerate(SBLK):
                    act.dma_start(shS[0:n, t, b, :], s[a:a + n, :]).then_inc(ffn_loaded, 16)
            act.dma_start(sdS, s_down).then_inc(ffn_loaded, 16)
            act.wait_ge(var_ready, 1)
            nc.scalar.activation(st[:, 3, :], st[:, 2, :], ACT.Sqrt).then_inc(std_ready, 1)
            for i, (_, dst, rows, cols) in enumerate(blocks):
                act.wait_ge(tr_full, i + 1)
                nc.scalar.activation(dst, T[i % 3][0:rows, 0:cols], ACT.Copy).then_inc(tr_taken, 1)
            for t, dst in enumerate((M, PV)):
                act.wait_ge(scaled_used, NCH * (t + 1))
                nc.scalar.activation(dst[:, 0:PIECE], R[0][:, :], ACT.Copy).then_inc(prod_taken, 1)
            act.wait_ge(gexp_ready, 1)
            nc.scalar.activation(comb[:, :, :], lg[:, :, :], ACT.Exp).then_inc(gexp_done, 1)
            for i in range(4):
                act.wait_ge(ct_full, i + 1)
                nc.scalar.activation(combT[:, i * 512:(i + 1) * 512], T[i % 2][0:PARTS, :], ACT.Copy)\
                    .then_inc(ct_taken, 1)
            for k in range(4 * NJ):
                m = SBLK[k % NJ - NPAIR][1] if k % NJ >= NPAIR else P
                act.wait_ge(gu_full, k + 1)
                if k >= 2:
                    act.wait_ge(h_ready, 2 * (k - 1))
                nc.scalar.activation(sg[0:m, k % 2, :], R[k % 2][0:m, 0:512], ACT.Silu).then_inc(gate_read, 1)

            k_sign = 0
            act.wait_ge(down_taken, 4)

            def exponent(n):
                q = n // 4
                wd_ = width(q)
                act.wait_ge(max_ready, q + 1)
                if n >= 3:
                    act.wait_ge(tp_full, tcount(n - 3))
                nc.scalar.activation(E[:, n % 3, 0:wd_], S[:, n % 8, 0:wd_], ACT.Exp,
                                     bias=mbias[:, q % 2, n % 4:n % 4 + 1], scale=UP).then_inc(exp_done, 1)

            def take_transposed(n):
                q = n // 4
                base = tcount(n) - len(tpieces(q))
                if n >= 2:
                    act.wait_ge(z_done, n - 1)
                    act.wait_ge(mem_kept, n - 1)
                for i, (a, b) in enumerate(tpieces(q)):
                    act.wait_ge(tp_full, base + i + 1)
                    nc.scalar.activation(PT[:, n % 2, a * P:b * P], T[(base + i) % 2][:, 0:(b - a) * P], ACT.Copy)\
                        .then_inc(tp_taken, 1)

            def keep_memory(n):
                q, nk = n // 4, n // 16 + 1
                act.wait_ge(tp_taken, tcount(n))
                if q >= 2:
                    act.wait_ge(ring_full, RING["out", q - 2] + 1)
                nc.scalar.activation(memPT[:, q % 2, n % 4, :], PT[0:MEM, n % 2, nk * P:(nk + 1) * P], ACT.Copy)\
                    .then_inc(mem_kept, 1)

            def take_z(q):
                act.wait_ge(z_done, 4 * (q + 1))
                if q >= 1:
                    act.wait_ge(ring_full, RING["out", q - 1] + 1)
                nc.scalar.activation(zst[:], Z[:, :], ACT.Copy).then_inc(z_taken, 1)

            def signs(u, s):
                nonlocal k_sign
                q = u // 2
                wd_ = width(q)
                if s == 0:
                    act.wait_ge(first_ready, q - FIRST + 1)
                    act.wait_ge(ring_taken, RING["score", 2 * u + 1, len(pieces(q)) - 1] + 1)
                else:
                    act.wait_ge(step_ready, STEP[u, s - 1] + 1)
                for h in (2 * (u % 2), 2 * (u % 2) + 1):
                    if k_sign >= 2:
                        act.wait_ge(signs_summed, k_sign - 1)
                    nc.scalar.activation(junk[:, k_sign % 2, 0:wd_], S[:, 4 * (q % 2) + h, 0:wd_], ACT.Sign,
                                         bias=tg[:, q % 2, s, 0, h:h + 1], scale=NUDGE,
                                         accum_out=tg[:, q % 2, s, 1, h:h + 1]).then_inc(signs_summed, 1)
                    k_sign += 1

            for p in range(QUADS + 3):
                for h in range(4):
                    m = 4 * (p - 2) + h
                    if 1 <= m <= 4 * QUADS:
                        exponent(m - 1)
                    if h == 2 and 0 <= p - 3:
                        take_z(p - 3)
                    if 2 <= m < 4 * QUADS + 2:
                        take_transposed(m - 2)
                    for k, (u, s) in enumerate(rounds_in(m)):
                        signs(u, s)
                        if k == 0 and 2 <= m < ACT_KEEPS + 2:
                            keep_memory(m - 2)
                    if not rounds_in(m) and 2 <= m < ACT_KEEPS + 2:
                        keep_memory(m - 2)

        @block.vector
        def _(dve):
            chain = [0]

            def link(ins):
                chain[0] += 1
                ins.then_inc(dve_chain, 1)
                dve.wait_ge(dve_chain, chain[0])

            V = nc.vector

            def bc(ap, n):
                return ap.rearrange("p (k o) -> p k o", o=1).to_broadcast([ap.shape[0], ap.shape[1], n])

            dve.wait_ge(x_loaded, 16)
            link(V.tensor_reduce(st[:, 0, :], acc[:, :, :], AXX, ALU.add))
            link(V.tensor_scalar(st[:, 0, :], st[:, 0, :], 1.0 / D, None, ALU.mult))
            link(V.tensor_tensor(XN[:, :, :], acc[:, :, :], bc(st[:, 0, :], D), ALU.subtract))
            link(V.tensor_tensor(xsq, XN[:, :, :], XN[:, :, :], ALU.mult))
            link(V.tensor_reduce(st[:, 1, :], xsq, AXX, ALU.add))
            V.tensor_scalar(st[:, 2, :], st[:, 1, :], 1.0 / D, EPS, ALU.mult, ALU.add).then_inc(var_ready, 1)
            dve.wait_ge(std_ready, 1)
            link(V.reciprocal(st[:, 4, :], st[:, 3, :]))
            link(V.tensor_tensor(st[:, 5, :], st[:, 4, :], st[:, 4, :], ALU.mult))
            link(V.tensor_tensor(st[:, 5, :], st[:, 5, :], st[:, 2, :], ALU.mult))
            link(V.tensor_scalar(st[:, 5, :], st[:, 5, :], -0.5, 1.5, ALU.mult, ALU.add))
            link(V.tensor_tensor(st[:, 4, :], st[:, 4, :], st[:, 5, :], ALU.mult))
            V.tensor_tensor(XN[:, :, :], XN[:, :, :], bc(st[:, 4, :], D), ALU.mult).then_inc(xn_ready, 1)
            dve.wait_ge(consts_loaded, 16 * 9)
            V.tensor_copy(identb[:], ident[:]).then_inc(casts_done, 1)
            V.tensor_copy(cmaskb[:], cmask[:]).then_inc(casts_done, 1)
            V.tensor_copy(selb, sel).then_inc(casts_done, 1)
            bo_rep = bob.rearrange("p (o d) -> p o d", o=1).to_broadcast([P, NB, D])
            link(V.tensor_tensor(acc[:, :, :], acc[:, :, :], bo_rep, ALU.add))

            dve.wait_ge(mixB_full, 1)
            link(V.tensor_scalar(preB.rearrange("p c k -> p (c k)"), R[0][:, 0:P], DH ** -0.5 * DOWN, None, ALU.mult))
            link(V.tensor_copy(postB.rearrange("p c k -> p (c k)"), R[0][:, P:2 * P]))
            for t in range(2):
                B = preB if t == 0 else postB
                for c in range(NCH):
                    k = NCH * t + c
                    if k >= 2:
                        dve.wait_ge(scaled_used, k - 1)
                    src = wT[:, 1, c, :] if t == 0 else woS[:, c, :]
                    if t == 0:
                        dve.wait_ge(tr_taken, n_att_tr)
                    else:
                        dve.wait_ge(att_loaded, 16 * 22)
                    V.tensor_tensor(scaledm[:, k % 2, :, :], bc(B[:, c, :], MEM),
                                    memT[:, t, c, :].rearrange("p (o m) -> p o m", o=1).to_broadcast([P, HEADS, MEM]),
                                    ALU.mult).then_inc(scaled_ready, 1)
                    V.tensor_tensor(scaled[:, k % 2, :, :], bc(B[:, c, :], D),
                                    src.rearrange("p (o n) -> p o n", o=1).to_broadcast([P, HEADS, D]),
                                    ALU.mult).then_inc(scaled_ready, 1)
                dve.wait_ge(scaled_used, NCH * (t + 1))
                if t == 0:
                    link(V.tensor_copy(M[:, PIECE:], R[1][:, :]))
                    link(V.tensor_copy(Kmem[:], T[0][:, 0:HEADS * MEM]))
                else:
                    V.tensor_copy(mvT, T[0][:, 0:HEADS * MEM]).then_inc(mvT_ready, 1)
                    link(V.tensor_copy(PV[:, PIECE:], R[1][:, :]))
                    dve.wait_ge(mv_full, 1)
                    for i in range(3):
                        link(V.tensor_copy(MV[:, i * 512:(i + 1) * 512], T[i][0:MEM, :]))
                    link(V.tensor_copy(MV[:, 1536:2048], Z[0:MEM, :]))
                dve.sem_inc(prod_taken, 1)

            dve.wait_ge(gates_full, 1)
            link(V.tensor_copy(lg[:, :, :], T[0][:, 0:NB * 17].rearrange("p (b e) -> p b e", b=NB)))
            dve.sem_inc(gates_taken, 1)
            lo16, down = lg[:, :, 0:EXPERTS], rt[:, 3, :, :]
            index = rt[:, 2, :, :]
            m1, m2 = st[:, 0, :], st[:, 1, :]
            for e in range(EXPERTS):
                link(V.memset(index[:, :, e:e + 1], float(EXPERTS - e)))
            for t, m in ((0, m1), (1, m2)):
                left = lo16 if t == 0 else down
                link(V.tensor_reduce(m, left, AXX, ALU.max))
                link(V.tensor_tensor(rt[:, t, :, :], left, bc(m, EXPERTS), ALU.is_equal))
                link(V.tensor_tensor(rt[:, t, :, :], rt[:, t, :, :], index, ALU.mult))
                link(V.tensor_reduce(st[:, 2, :], rt[:, t, :, :], AXX, ALU.max))
                link(V.tensor_tensor(rt[:, t, :, :], index, bc(st[:, 2, :], EXPERTS), ALU.is_equal))
                if t == 0:
                    link(V.scalar_tensor_tensor(out=down, in0=rt[:, 0, :, :], scalar=LOWEST, in1=lo16,
                                                op0=ALU.mult, op1=ALU.add))
            link(V.tensor_tensor(rt[:, 0, :, :], rt[:, 0, :, :], rt[:, 1, :, :], ALU.add))
            link(V.tensor_tensor(lo16, lo16, bc(m1, EXPERTS), ALU.subtract))
            V.tensor_scalar(lg[:, :, 16:17], lg[:, :, 16:17], -1.0, None, ALU.mult).then_inc(gexp_ready, 1)
            dve.wait_ge(gexp_done, 1)
            ce = comb[:, :, 0:EXPERTS]
            link(V.tensor_tensor(ce, ce, rt[:, 0, :, :], ALU.mult))
            link(V.tensor_reduce(st[:, 2, :], ce, AXX, ALU.add))
            link(V.reciprocal(st[:, 3, :], st[:, 2, :]))
            link(V.tensor_tensor(ce, ce, bc(st[:, 3, :], EXPERTS), ALU.mult))
            link(V.tensor_scalar(comb[:, :, 16:17], comb[:, :, 16:17], 1.0, None, ALU.add))
            link(V.reciprocal(comb[:, :, 16:17], comb[:, :, 16:17]))
            for i in range(3):
                part = parts3[:, :, 17 * i:17 * (i + 1)]
                link(V.tensor_copy(partb, comb[:, :, :]))
                link(V.tensor_copy(part, partb))
                if i < 2:
                    link(V.tensor_tensor(comb[:, :, :], comb[:, :, :], part, ALU.subtract))
            dve.sem_inc(comb_ready, 1)

            for c in range(4):
                for j in range(NJ):
                    k = NJ * c + j
                    m = SBLK[j - NPAIR][1] if j >= NPAIR else P
                    dve.wait_ge(gate_read, k + 1)
                    if c >= 1:
                        dve.wait_ge(down_full, c)
                    V.tensor_tensor(su[0:m, k % 2, :], sg[0:m, k % 2, :], R[k % 2][0:m, 512:1024], ALU.mult)\
                        .then_inc(h_ready, 1)
                    dve.wait_ge(h_ready, 2 * k + 1)
                    V.tensor_tensor(H[0:m, j, :], su[0:m, k % 2, :], T[k % 2][0:m, :], ALU.mult).then_inc(h_ready, 1)
                dve.wait_ge(down_full, c + 1)
                V.tensor_tensor(acc[:, 4 * c:4 * c + 4, :], acc[:, 4 * c:4 * c + 4, :],
                                Z[:, :].rearrange("p (b d) -> p b d", b=4), ALU.add).then_inc(down_taken, 1)
            dve.wait_ge(down_taken, 4)
            for i in range(3):
                V.memset(T[i][:, :], 0.0).then_inc(t_banks_zeroed, 1)

            def general(n, target, link_):
                wd_ = width(n // 4)
                src = S[:, n % 8, 0:wd_]
                for i in range(TOPK // 8):
                    link_(V.max(t8[:], src))
                    if i < TOPK // 8 - 1:
                        link_(V.match_replace(out=Y[:, 0:wd_], in_to_replace=t8[:], in_values=src, imm_value=LOWEST))
                        src = Y[:, 0:wd_]
                link_(V.tensor_copy(target, t8[:, 7:8]))

            def take_scores(n):
                q = n // 4
                if q >= 2:
                    dve.wait_ge(probs_ready, n - 7)
                for i, (a, b) in enumerate(pieces(q)):
                    k = RING["score", n, i]
                    dve.wait_ge(ring_full, k + 1)
                    V.tensor_scalar(S[:, n % 8, a:b], R[k % 2][:, 0:b - a], 1.0, LOWEST, ALU.mult, ALU.max,
                                    accum_out=mxp[:, n % 8, i:i + 1]).then_inc(ring_taken, 1)

            def maxima(q):
                b = q % 2
                np_ = len(pieces(q))
                dve.wait_ge(ring_taken, RING["score", 4 * q + 3, np_ - 1] + 1)
                if q >= 2:
                    dve.wait_ge(exp_done, 4 * (q - 1))
                link(V.tensor_reduce(mxq[:, b, :], mxp[:, 4 * b:4 * b + 4, 0:np_], AXX, ALU.max))
                V.tensor_scalar(mbias[:, b, :], mxq[:, b, :], -UP, None, ALU.mult).then_inc(max_ready, 1)

            def take_queries(q):
                k = RING["query", q]
                dve.wait_ge(ring_full, k + 1)
                if needs_search(q - 2):
                    dve.wait_ge(squares_ready, q - 2 - FIRST + 1)
                V.tensor_copy(QT[:, q % 2, :], R[k % 2][:, 0:512]).then_inc(ring_taken, 1)

            def take_squares(q):
                k = SMALL["squares", q]
                dve.wait_ge(small_full, k + 1)
                if q >= FIRST + 2:
                    dve.wait_ge(first_ready, q - 2 - FIRST + 1)
                V.tensor_copy(sg2[:, q % 2, :], F[:, 0:4]).then_inc(small_taken, 1)

            def take_failures(u):
                k = SMALL["failures", u]
                dve.wait_ge(small_full, k + 1)
                V.tensor_copy(failed[:], F[0:1, 0:5]).then_inc(small_taken, 1)
                dve.wait_ge(small_taken, k + 1)

            def marks(u):
                q, c = u // 2, 2 * (u % 2)
                b, c, i = q % 2, slice(c, c + 2), u % 2
                nt = tg[:, b, ROUNDS - 1, 0, c]
                dve.wait_ge(step_ready, STEP[u, ROUNDS - 2] + 1)
                if u >= 2 * FIRST + 2:
                    dve.wait_ge(fails_ready, 2 * (u - 2 * FIRST - 1))
                link(V.tensor_scalar(beyond[:, i, :], nt, -NEXT, None, ALU.mult))
                V.tensor_scalar(shift[:, i, :], nt, 0.0, 0.5, ALU.is_gt, ALU.mult).then_inc(mark_steps, 1)
                V.scalar_tensor_tensor(out=y17[:, b, c, 0], in0=nt, scalar=-1.0, in1=beyond[:, i, :],
                                       op0=ALU.mult, op1=ALU.max).then_inc(mark_steps, 1)
                V.scalar_tensor_tensor(out=mark[:, b, c], in0=nt, scalar=-1.0, in1=beyond[:, i, :],
                                       op0=ALU.mult, op1=ALU.min).then_inc(mark_steps, 1)
                dve.wait_ge(mark_steps, 3 * (u - 2 * FIRST) + 3)
                link(V.tensor_scalar(shift[:, i, :], shift[:, i, :], TOPK - width(q) / 2 - 0.25, None, ALU.add))
                V.tensor_tensor(tiny[:, i, :], y17[:, b, c, 0], mark[:, b, c], ALU.is_equal).then_inc(marks_set, 1)

            def rank_of(u):
                q, c = u // 2, slice(2 * (u % 2), 2 * (u % 2) + 2)
                dve.wait_ge(signs_summed, 2 * (TURN[u, ROUNDS - 1] + 1))
                dve.wait_ge(marks_set, u - 2 * FIRST + 1)
                V.scalar_tensor_tensor(out=rank[:, c], in0=tg[:, q % 2, ROUNDS - 1, 1, c], scalar=-0.5,
                                       in1=shift[:, u % 2, :], op0=ALU.mult, op1=ALU.add).then_inc(rank_steps, 1)

            def rank_offsets(u):
                q, c = u // 2, slice(2 * (u % 2), 2 * (u % 2) + 2)
                dve.wait_ge(rank_steps, 6 * (u - 2 * FIRST) + 1)
                for i, centre in enumerate((4.0, 8.0)):
                    V.tensor_scalar(off[:, i, :], rank[:, c], centre, None, ALU.subtract).then_inc(rank_steps, 1)
                V.tensor_tensor(hot[:, q % 2, c, :], iota[:, c, :], bc(rank[:, c], 17), ALU.subtract)\
                    .then_inc(rank_steps, 1)

            def rank_tests(u):
                q, c = u // 2, slice(2 * (u % 2), 2 * (u % 2) + 2)
                h = hot[:, q % 2, c, :]
                dve.wait_ge(rank_steps, 6 * (u - 2 * FIRST) + 4)
                V.tensor_tensor(off[:, :, :], off[:, :, :], off[:, :, :], ALU.mult).then_inc(rank_steps, 1)
                V.tensor_tensor(h, h, h, ALU.mult).then_inc(rank_steps, 1)
                dve.wait_ge(rank_steps, 6 * (u - 2 * FIRST) + 6)
                if u >= 2 * FIRST + 2:
                    dve.wait_ge(small_full, SMALL["failures", u - 2] + 1)
                for i, far_ in enumerate((4.5 ** 2, 8.5 ** 2)):
                    V.scalar_tensor_tensor(out=fail[:, u % 2, 2 * i:2 * i + 2], in0=off[:, i, :], scalar=far_,
                                           in1=tiny[:, u % 2, :], op0=ALU.is_gt, op1=ALU.add).then_inc(fails_ready, 1)
                V.tensor_scalar(h, h, 0.25, None, ALU.is_lt).then_inc(ranks_ready, 1)

            def lower(n):
                q = n // 4
                s = S[:, n % 8, 0:width(q)]
                return V.scalar_tensor_tensor(out=Y[:, 0:width(q)], in0=s, scalar=mark[:, q % 2, n % 4:n % 4 + 1],
                                              in1=s, op0=ALU.is_gt, op1=ALU.subtract, reverse1=True)

            def below(n):
                dve.wait_ge(mark_steps, 3 * (n // 2 - 2 * FIRST) + 3)
                if n > 4 * FIRST:
                    dve.wait_ge(largest_found, n - 4 * FIRST)
                lower(n).then_inc(lowered, 1)

            def largest(n):
                q = n // 4
                dve.wait_ge(lowered, n - 4 * FIRST + 1)
                V.max(y17[:, q % 2, n % 4, 1:9], Y[:, 0:width(q)]).then_inc(largest_found, 1)

            def choose(n):
                q = n // 4
                dve.wait_ge(ranks_ready, n // 2 - 2 * FIRST + 1)
                dve.wait_ge(largest_found, n - 4 * FIRST + 1)
                V.scalar_tensor_tensor(out=pick[:, n % 2, 0:9], in0=y17[:, q % 2, n % 4, 0:9], scalar=1.0,
                                       in1=hot[:, q % 2, n % 4, 0:9], op0=ALU.mult, op1=ALU.mult,
                                       accum_out=thr[:, n % 8:n % 8 + 1]).then_inc(chosen, 1)

            def repair(n, any_failed):
                q, b, h = n // 4, (n // 4) % 2, n % 4
                wd_ = width(q)
                with dve.If(any_failed > 0):
                    i = n % 2
                    beyond_9 = dve.value_load(failed[0:1, i:i + 1], min_val=0, max_val=2 * P)
                    with dve.If(beyond_9 > 0):
                        steps = [0]

                        def glink(ins):
                            steps[0] += 1
                            ins.then_inc(general_chain, 1)
                            dve.wait_ge(general_chain, steps[0])

                        dve.wait_ge(chosen, n - 4 * FIRST + 1)
                        glink(lower(n))
                        glink(V.match_replace(out=Y[:, 0:wd_], in_to_replace=y17[:, b, h, 1:9],
                                              in_values=Y[:, 0:wd_], imm_value=LOWEST))
                        glink(V.max(y17[:, b, h, 9:17], Y[:, 0:wd_]))
                        glink(V.scalar_tensor_tensor(out=pick[:, n % 2, :], in0=y17[:, b, h, :], scalar=1.0,
                                                     in1=hot[:, b, h, :], op0=ALU.mult, op1=ALU.mult,
                                                     accum_out=thr[:, n % 8:n % 8 + 1]))
                        dve.sem_clear(general_chain)
                        beyond_17 = dve.value_load(failed[0:1, 2 + i:3 + i], min_val=0, max_val=2 * P)
                        with dve.If(beyond_17 > 0):
                            steps[0] = 0
                            general(n, thr[:, n % 8:n % 8 + 1], glink)
                            dve.sem_clear(general_chain)

            def weights(n):
                wd_ = width(n // 4)
                dve.wait_ge(exp_done, n + 1)
                if n >= 4 * FIRST:
                    dve.wait_ge(chosen, n - 4 * FIRST + 1)
                V.scalar_tensor_tensor(out=E[:, n % 3, 0:wd_], in0=S[:, n % 8, 0:wd_],
                                       scalar=thr[:, n % 8:n % 8 + 1], in1=E[:, n % 3, 0:wd_],
                                       op0=ALU.is_ge, op1=ALU.mult, accum_out=rsum[:, n % 8:n % 8 + 1])\
                    .then_inc(probs_ready, 1)

            def inverse(q):
                dve.wait_ge(probs_ready, 4 * (q + 1))
                V.reciprocal(rinv[:, q % 2, :], rsum[:, 4 * (q % 2):4 * (q % 2) + 4]).then_inc(inverted, 1)

            def add_out(q, h):
                k = RING["out", q]
                b = q // 4
                dve.wait_ge(ring_full, k + 1)
                if h == 0:
                    dve.wait_ge(inverted, q + 1)
                else:
                    dve.wait_ge(added, 3 * q + h)
                ins = V.scalar_tensor_tensor(out=acc[:, b, :], in0=R[k % 2][:, h * D:(h + 1) * D],
                                             scalar=rinv[:, q % 2, h:h + 1], in1=acc[:, b, :],
                                             op0=ALU.mult, op1=ALU.add)
                if h < 3:
                    ins.then_inc(added, 1)
                else:
                    ins.then_inc(ring_taken, 1)
                    dve.wait_ge(ring_taken, k + 1)
                    if q % 4 == 3:
                        dve.sem_inc(rows_ready, 1)

            take_queries(0)
            for p in range(QUADS + 3):
                q = p - 2
                search = needs_search(q)
                for h in range(4):
                    m = 4 * q + h
                    first_of_pair = search and h % 2 == 0
                    if first_of_pair:
                        marks(m // 2)
                    if search:
                        below(m)
                    if 2 <= m < 4 * QUADS + 2:
                        weights(m - 2)
                    if first_of_pair:
                        rank_of(m // 2)
                    if search:
                        largest(m)
                    if first_of_pair:
                        rank_offsets(m // 2)
                    if 0 <= m + 6 < 4 * QUADS:
                        take_scores(m + 6)
                    if first_of_pair:
                        rank_tests(m // 2)
                    if h == 1 and 0 <= p - 1 < QUADS:
                        maxima(p - 1)
                    if h == 2 and 0 <= p - 3:
                        inverse(p - 3)
                    if h == 2 and p + 1 < QUADS:
                        take_queries(p + 1)
                    if h % 2 == 1 and search:
                        take_failures(m // 2)
                        any_failed = dve.value_load(failed[0:1, 4:5], min_val=0, max_val=4 * P)
                        for n in (m - 1, m):
                            choose(n)
                        for n in (m - 1, m):
                            repair(n, any_failed)
                    if h == 1 and needs_search(p):
                        take_squares(p)
                    if not search and 0 <= m < 4 * QUADS:
                        general(m, thr[:, m % 8:m % 8 + 1], link)
                    if h == 3 and 0 <= p - 3:
                        for i in range(4):
                            add_out(p - 3, i)

        @block.tensor
        def _(pe):
            mm, tr = nc.tensor.matmul, nc.tensor.transpose

            pe.wait_ge(consts_loaded, 16 * 9)
            for i, (parts, _, _, _) in enumerate(blocks):
                if i == 0:
                    pe.wait_ge(att_loaded, 16 * 22)
                if i == n_att_tr:
                    pe.wait_ge(ffn_loaded, 16 * 12)
                if i == n_w_tr:
                    pe.wait_ge(xn_ready, 1)
                if i >= 3:
                    pe.wait_ge(tr_taken, i - 2)
                at = 0
                for src, rows, cols in parts:
                    last = tr(T[i % 3][0:cols, at:at + rows], src, ident[0:rows, 0:rows])
                    at += rows
                last.then_inc(tr_full, 1)
            pe.wait_ge(tr_taken, n_att_tr)
            for t, m in enumerate((preS, postT)):
                for c in range(NCH):
                    last = mm(R[0][:, t * P + c * 16:t * P + (c + 1) * 16], sel[0:HEADS, c, :], m, start=True, stop=True)
            last.then_inc(mixB_full, 1)
            pe.wait_ge(tr_taken, n_tr)
            ready = 0
            for t in range(2):
                if t == 1:
                    pe.wait_ge(prod_taken, 2)
                for c in range(NCH):
                    k = NCH * t + c
                    ready += 2
                    pe.wait_ge(scaled_ready, ready)
                    lhs = wT[:, 0, c, :] if t == 0 else wT[:, 2, c, :]
                    for i in range(4):
                        last = mm(R[i // 2][:, (i % 2) * 512:(i % 2 + 1) * 512], lhs,
                                  scaled[:, k % 2, 4 * i:4 * i + 4, :].rearrange("p k n -> p (k n)"),
                                  start=(c == 0), stop=(c == NCH - 1))
                    last = mm(T[0][:, 0:HEADS * MEM], lhs if t == 0 else woS[:, c, :],
                              scaledm[:, k % 2, :, :].rearrange("p k m -> p (k m)"),
                              start=(c == 0), stop=(c == NCH - 1))
                    last.then_inc(scaled_used, 1)
            pe.wait_ge(mvT_ready, 1)
            for h in range(HEADS):
                bank = T[h // 4] if h < 12 else Z
                last = tr(bank[0:MEM, h % 4 * P:(h % 4 + 1) * P], mvT[:, h * MEM:(h + 1) * MEM], ident[:, :])
            last.then_inc(mv_full, 1)
            pe.wait_ge(prod_taken, 4)
            for b in range(NB):
                last = mm(T[0][:, 17 * b:17 * (b + 1)], xnT[:, b * P:(b + 1) * P], gateT, start=True, stop=True)
            last.then_inc(gates_full, 1)
            pe.wait_ge(comb_ready, 1)
            pe.wait_ge(gates_taken, 1)
            for i in range(4):
                if i >= 2:
                    pe.wait_ge(ct_taken, i - 1)
                for b in range(4):
                    last = tr(T[i % 2][0:PARTS, b * P:(b + 1) * P], parts3[:, 4 * i + b, :], ident[:, :])
                last.then_inc(ct_full, 1)
            pe.wait_ge(ct_taken, 4)
            for c in range(4):
                cols = xnT[:, c * 512:(c + 1) * 512]
                for j in range(NJ):
                    k = NJ * c + j
                    if j < NPAIR:
                        m = P
                        lg_, lu_ = (a[:, 2 * j:2 * j + 2, :].rearrange("p e f -> p (e f)") for a in (wg, wu))
                        ls_ = selb[:, j, :]
                    else:
                        a0, m = SBLK[j - NPAIR]
                        lg_, lu_ = (shT[:, t, j - NPAIR, 0:m] for t in range(2))
                        ls_ = selb[:, NPAIR, 0:m]
                    if k >= 2:
                        pe.wait_ge(h_ready, 2 * (k - 1))
                    mm(R[k % 2][0:m, 0:512], lg_, cols, start=True, stop=True)
                    mm(R[k % 2][0:m, 512:1024], lu_, cols, start=True, stop=True)
                    mm(T[k % 2][0:m, :], ls_, combT[:, c * 512:(c + 1) * 512], start=True, stop=True)\
                        .then_inc(gu_full, 1)
                pe.wait_ge(h_ready, 2 * NJ * (c + 1))
                if c >= 1:
                    pe.wait_ge(down_taken, c)
                for b in range(4):
                    for j in range(NJ):
                        m = SBLK[j - NPAIR][1] if j >= NPAIR else P
                        rhs = wd[:, j, :] if j < NPAIR else sdT[0:m, j - NPAIR, :]
                        last = mm(Z[:, b * D:(b + 1) * D], H[0:m, j, b * P:(b + 1) * P], rhs,
                                  start=(j == 0), stop=(j == NJ - 1))
                last.then_inc(down_full, 1)

            pe.wait_ge(down_taken, 4)
            pe.wait_ge(t_banks_zeroed, 3)
            pe.wait_ge(casts_done, 3)
            pe.wait_ge(ones_set, 1)

            def slot(item):
                k = RING[item]
                if k >= 2:
                    pe.wait_ge(ring_taken, k - 1)
                return R[k % 2]

            def queries(q):
                r, ps = q // 4, slot(("query", q))
                for h in range(4):
                    k = 4 * (q % 4) + h
                    last = mm(ps[:, h * P:(h + 1) * P], M[:, k * D:(k + 1) * D], xnT[:, r * P:(r + 1) * P],
                              start=True, stop=True)
                last.then_inc(ring_full, 1)

            def small_slot(item):
                if SMALL[item] > 0:
                    pe.wait_ge(small_taken, SMALL[item])

            def squares(q):
                small_slot(("squares", q))
                pe.wait_ge(squares_ready, q - FIRST + 1)
                for h in range(4):
                    last = mm(F[:, h:h + 1], sq[:, h * P:(h + 1) * P], ones[:, 0:1], start=True, stop=True)
                last.then_inc(small_full, 1)

            def failures(u):
                small_slot(("failures", u))
                pe.wait_ge(fails_ready, 2 * (u - 2 * FIRST + 1))
                mm(F[0:1, 0:4], ones[:, 0:1], fail[:, u % 2, :], start=True, stop=True)
                for h in range(2):
                    last = mm(F[0:1, 4:5], ones[:, 0:1], fail[:, u % 2, h:h + 1], start=(h == 0), stop=(h == 1))
                last.then_inc(small_full, 1)

            def scores(n):
                q, r, h = n // 4, n // 16, n % 4
                keys = P * (r + 1)
                if h == 0:
                    pe.wait_ge(ring_taken, RING["query", q] + 1)
                for i, (a, b) in enumerate(pieces(q)):
                    ps = slot(("score", n, i))
                    for s in range(a, b, 512):
                        e = min(s + 512, b)
                        ek = min(e, keys)
                        if ek > s:
                            diag = s <= r * P < ek
                            last = mm(ps[:, s - a:ek - a], QT[:, q % 2, h * P:(h + 1) * P], xnT[:, s:ek],
                                      start=True, stop=not diag)
                            if diag:
                                last = mm(ps[:, r * P - a:keys - a], identb[:], cmaskb[:], start=False, stop=True)
                        if e > keys:
                            k = n % 16
                            last = mm(ps[:, keys - a:e - a], xnT[:, r * P:(r + 1) * P], Kmem[:, k * MEM:(k + 1) * MEM],
                                      start=True, stop=True)
                    last.then_inc(ring_full, 1)

            def transposes(n, first, end):
                q = n // 4
                nk = q // 4 + 1
                base = tcount(n) - len(tpieces(q))
                if first == 0:
                    pe.wait_ge(probs_ready, n + 1)
                for i, (a, b) in list(enumerate(tpieces(q)))[first:end]:
                    if base + i >= 2:
                        pe.wait_ge(tp_taken, base + i - 1)
                    for j in range(a, b):
                        cols = P if j < nk else MEM
                        last = tr(T[(base + i) % 2][0:cols, (j - a) * P:(j - a + 1) * P],
                                  E[:, n % 3, j * P:j * P + cols], ident[:])
                    last.then_inc(tp_full, 1)

            def values(n):
                q, h = n // 4, n % 4
                nk = q // 4 + 1
                if h == 0 and q >= 1:
                    pe.wait_ge(z_taken, q)
                pe.wait_ge(tp_taken, tcount(n))
                for j in range(nk):
                    last = mm(Z[:, h * P:(h + 1) * P], XN[:, j, :], PT[:, n % 2, j * P:(j + 1) * P],
                              start=(j == 0), stop=(j == nk - 1))
                last.then_inc(z_done, 1)

            def project(q):
                ps = slot(("out", q))
                pe.wait_ge(z_taken, q + 1)
                pe.wait_ge(mem_kept, 4 * (q + 1))
                for h in range(4):
                    k = 4 * (q % 4) + h
                    mm(ps[:, h * D:(h + 1) * D], zst[:, h * P:(h + 1) * P], PV[:, k * D:(k + 1) * D],
                       start=True, stop=False)
                    last = mm(ps[:, h * D:(h + 1) * D], memPT[:, q % 2, h, :], MV[:, k * D:(k + 1) * D],
                              start=False, stop=True)
                last.then_inc(ring_full, 1)

            queries(0)
            for p in range(QUADS + 3):
                for h in range(4):
                    m = 4 * (p - 2) + h
                    turn = 2 <= m < 4 * QUADS + 2
                    if turn:
                        transposes(m - 2, 0, 2)
                    if h == 1 and needs_search(p):
                        squares(p)
                    if h == 2 and p + 1 < QUADS:
                        queries(p + 1)
                    if h == 3 and 0 <= p - 3:
                        project(p - 3)
                    wait_last = m + 7 < 4 * QUADS and len(pieces((m + 7) // 4)) > 2
                    if turn:
                        transposes(m - 2, 2, 5)
                    if 0 <= m + 7 < 4 * QUADS and not wait_last:
                        scores(m + 7)
                    if turn:
                        values(m - 2)
                    if h % 2 == 0 and needs_search(p - 2):
                        failures(m // 2)
                    if wait_last:
                        scores(m + 7)


_INS = ["L0_attn_x", "L0_attn_Wq", "L0_attn_Wk", "L0_attn_Wv", "L0_attn_pre_proj", "L0_attn_post_proj",
        "L0_attn_mem_k", "L0_attn_mem_v", "L0_attn_Wo", "L0_attn_bo", "L0_ffn_gate_w", "L0_ffn_w_gate_up",
        "L0_ffn_w_down", "L0_ffn_shared_w_gate", "L0_ffn_shared_w_up", "L0_ffn_shared_w_down",
        "L0_ffn_shared_gate_w"]


def shape_tables():
    import numpy as np

    def over(z):
        return 0.5 * math.erfc(z / math.sqrt(2.0))

    def density(z):
        return math.exp(-z * z / 2) / math.sqrt(2 * math.pi)

    sel = np.zeros((EXPERTS + 1, 9, P), np.float32)
    for c in range(8):
        for p in range(P):
            sel[2 * c + p // DH, c, p] = 1.0
    sel[EXPERTS, 8, :] = 1.0
    i = np.arange(P)
    cmask = np.where(i[None, :] > i[:, None], np.float32(MASKED), np.float32(0.0)).astype(np.float32)
    spread = 4.6
    z = np.zeros(N)
    kap = np.ones(N)
    for r in range(P, N):
        lo, hi = -2.0, 5.0
        for _ in range(40):
            mid = (lo + hi) / 2
            above = (r + 1) * over(mid) + MEM * over(mid / spread)
            lo, hi = (mid, hi) if above > AIM else (lo, mid)
        z[r] = mid
        kap[r] = 0.5 / ((r + 1) * density(mid) + MEM * density(mid / spread) / spread)
    return {"ident": np.eye(P, dtype=np.float32), "sel": sel.reshape(EXPERTS + 1, 9 * P), "cmask": cmask,
            "nz": np.ascontiguousarray(-z.reshape(NB, P).T).astype(np.float32),
            "kap": np.ascontiguousarray(kap.reshape(NB, P).T).astype(np.float32),
            "iota": np.tile(np.arange(17, dtype=np.float32), (P, 4))}


def kernel(**inputs):
    import numpy as np
    import concourse.bacc as bacc
    from concourse.bass_utils import run_bass_kernel_spmd

    nc = bacc.Bacc("TRN2", target_bir_lowering=False, num_devices=1)
    arrays = {f"in_{n}": np.ascontiguousarray(inputs[n]) for n in _INS}
    arrays["in_L0_attn_x"] = arrays["in_L0_attn_x"].reshape(N, D)
    arrays.update({f"tab_{k}": v for k, v in shape_tables().items()})
    args = [nc.dram_tensor(k, v.shape, mybir.dt.from_np(v.dtype), kind="ExternalInput").ap()
            for k, v in arrays.items()]
    out = nc.dram_tensor("out_y", (N, D), F32, kind="ExternalOutput").ap()
    build(nc, *args, out)
    r = run_bass_kernel_spmd(nc, [arrays], core_ids=[0])
    return r.results[0]["out_y"].reshape(1, N, D)
```
